# Optimizing a Trainium2 kernel written in Bass

```python
import numpy as np
import jax
import jax.numpy as jnp

def _softmax(x, axis=-1):
    return jax.nn.softmax(x, axis=axis)

def _gelu(x):
    return jax.nn.gelu(x, approximate=True)

def _silu(x):
    return jax.nn.silu(x)

def _sigmoid(x):
    return jax.nn.sigmoid(x)

def _layernorm(x, axis=-1, eps=1e-05):
    m = jnp.mean(x, axis=axis, keepdims=True)
    v = jnp.var(x, axis=axis, keepdims=True)
    return (x - m) / jnp.sqrt(v + eps)

def _scatter_add(tgt, idx, src, axis=0):
    return tgt.at[idx].add(src)

def _segment_sum(src, seg, n):
    return jax.ops.segment_sum(src, seg, n)
kernel_name = 'mk_gnn_resnorm_d2_gnn_r8_ebab64'

def setup_inputs(seed: int=0):
    np.random.seed(seed)
    _w = jnp.asarray

    def _rec_inputs():
        import jax
        import jax.numpy as jnp
        _gk = jax.random.key(seed)
        x = -0.0001006 + 1 * jax.random.normal(jax.random.fold_in(_gk, 1), (12500, 96), jnp.float32)
        src = jax.random.randint(jax.random.fold_in(_gk, 2), (200000,), 0, 12500, jnp.int32)
        dst = jax.random.randint(jax.random.fold_in(_gk, 3), (200000,), 0, 12500, jnp.int32)
        _o = jnp.argsort(dst, stable=True)
        src = src[_o]
        dst = dst[_o]
        edge_attr_17 = jax.random.uniform(jax.random.fold_in(_gk, 11), (200000, 17), jnp.float32, 0.0, 1)
        edge_attr_32 = 0.000196303 + 1.00016 * jax.random.normal(jax.random.fold_in(_gk, 12), (200000, 32), jnp.float32)
        return (x, src, dst, edge_attr_17, edge_attr_32)
    x, src, dst, edge_attr_17, edge_attr_32 = _rec_inputs()

    def _L0_gnn_setup():
        import jax, jax.numpy as jnp
        import numpy as np
        N_NODES = 6250
        N_EDGES = 100000
        IN_DIM = 96
        OUT_DIM = 96
        EDGE_DIM = 32
        BN_EPS = 1e-05
        key = jax.random.key(seed)
        ks = jax.random.split(key, 12)
        x = jax.random.normal(ks[0], (N_NODES, IN_DIM), dtype=jnp.float32)
        edge_index = jax.random.randint(ks[1], (2, N_EDGES), 0, N_NODES, dtype=jnp.int64)
        edge_attr = jax.random.normal(ks[2], (N_EDGES, EDGE_DIM), dtype=jnp.float32)
        We = jax.random.normal(ks[3], (EDGE_DIM, IN_DIM), dtype=jnp.float32) / np.sqrt(EDGE_DIM)
        be = jnp.zeros((IN_DIM,), dtype=jnp.float32)
        W1 = jax.random.normal(ks[4], (IN_DIM, OUT_DIM), dtype=jnp.float32) / np.sqrt(IN_DIM)
        b1 = jnp.zeros((OUT_DIM,), dtype=jnp.float32)
        W2 = jax.random.normal(ks[5], (OUT_DIM, OUT_DIM), dtype=jnp.float32) / np.sqrt(OUT_DIM)
        b2 = jnp.zeros((OUT_DIM,), dtype=jnp.float32)
        gamma = jnp.ones((OUT_DIM,), dtype=jnp.float32)
        beta = jnp.zeros((OUT_DIM,), dtype=jnp.float32)
        return {'x': x, 'edge_index': edge_index, 'edge_attr': edge_attr, 'We': We, 'be': be, 'W1': W1, 'b1': b1, 'W2': W2, 'b2': b2, 'gamma': gamma, 'beta': beta}
    _L0_gnn_all = _L0_gnn_setup()
    _L0_gnn_in = {k: v for k, v in _L0_gnn_all.items() if k in ('We', 'be', 'W1', 'b1', 'W2', 'b2', 'gamma', 'beta')}
    del _L0_gnn_all

    def _L1_gnn_setup():
        import jax, jax.numpy as jnp
        import numpy as np
        N = 6250
        E = 100000
        D = 96
        ED = 17
        key = jax.random.key(seed)
        ks = jax.random.split(key, 12)
        x = jax.random.normal(ks[0], (N, D), dtype=jnp.float32)
        edge_index = jax.random.randint(ks[1], (2, E), 0, N, dtype=jnp.int64)
        edge_attr = jax.random.uniform(ks[2], (E, ED), dtype=jnp.float32)
        s = 1.0 / np.sqrt(ED)
        W1 = jax.random.uniform(ks[3], (D, ED), jnp.float32, -s, s)
        b1 = jax.random.uniform(ks[4], (D,), jnp.float32, -s, s)
        s = 1.0 / np.sqrt(D)
        W2 = jax.random.uniform(ks[5], (D, D), jnp.float32, -s, s)
        b2 = jax.random.uniform(ks[6], (D,), jnp.float32, -s, s)
        Ws = jax.random.uniform(ks[7], (D, D), jnp.float32, -s, s)
        bs = jax.random.uniform(ks[8], (D,), jnp.float32, -s, s)
        Wn = jax.random.uniform(ks[9], (D, D), jnp.float32, -s, s)
        bn = jax.random.uniform(ks[10], (D,), jnp.float32, -s, s)
        return {'x': x, 'edge_index': edge_index, 'edge_attr': edge_attr, 'W1': W1, 'b1': b1, 'W2': W2, 'b2': b2, 'Ws': Ws, 'bs': bs, 'Wn': Wn, 'bn': bn}
    _L1_gnn_all = _L1_gnn_setup()
    _L1_gnn_in = {k: v for k, v in _L1_gnn_all.items() if k in ('W1', 'b1', 'W2', 'b2', 'Ws', 'bs', 'Wn', 'bn')}
    del _L1_gnn_all
    return {'x': x, 'src': src, 'dst': dst, 'edge_attr_17': edge_attr_17, 'edge_attr_32': edge_attr_32, 'L0_gnn_We': _L0_gnn_in['We'], 'L0_gnn_be': _L0_gnn_in['be'], 'L0_gnn_W1': _L0_gnn_in['W1'], 'L0_gnn_b1': _L0_gnn_in['b1'], 'L0_gnn_W2': _L0_gnn_in['W2'], 'L0_gnn_b2': _L0_gnn_in['b2'], 'L0_gnn_gamma': _L0_gnn_in['gamma'], 'L0_gnn_beta': _L0_gnn_in['beta'], 'L1_gnn_W1': _L1_gnn_in['W1'], 'L1_gnn_b1': _L1_gnn_in['b1'], 'L1_gnn_W2': _L1_gnn_in['W2'], 'L1_gnn_b2': _L1_gnn_in['b2'], 'L1_gnn_Ws': _L1_gnn_in['Ws'], 'L1_gnn_bs': _L1_gnn_in['bs'], 'L1_gnn_Wn': _L1_gnn_in['Wn'], 'L1_gnn_bn': _L1_gnn_in['bn']}

def reference(x, src, dst, edge_attr_17, edge_attr_32, L0_gnn_We, L0_gnn_be, L0_gnn_W1, L0_gnn_b1, L0_gnn_W2, L0_gnn_b2, L0_gnn_gamma, L0_gnn_beta, L1_gnn_W1, L1_gnn_b1, L1_gnn_W2, L1_gnn_b2, L1_gnn_Ws, L1_gnn_bs, L1_gnn_Wn, L1_gnn_bn):
    import jax
    import jax.numpy as jnp

    def _L0_gnn_ref(x, edge_index, edge_attr, We, be, W1, b1, W2, b2, gamma, beta):
        import jax, jax.numpy as jnp
        import numpy as np
        N_NODES = 6250
        N_EDGES = 100000
        IN_DIM = 96
        OUT_DIM = 96
        EDGE_DIM = 32
        BN_EPS = 1e-05
        src = edge_index[0]
        dst = edge_index[1]
        msg = jax.nn.relu(x[src] + edge_attr @ We + be)
        aggr = jax.ops.segment_sum(msg, dst, num_segments=x.shape[0])
        h = x + aggr
        h = jax.nn.relu(h @ W1 + b1) @ W2 + b2
        mean = jnp.mean(h, axis=0)
        var = jnp.mean(jnp.square(h - mean), axis=0)
        h = (h - mean) * jax.lax.rsqrt(var + BN_EPS) * gamma + beta
        return jax.nn.relu(h)

    def _L1_gnn_ref(x, edge_index, edge_attr, W1, b1, W2, b2, Ws, bs, Wn, bn):
        import jax, jax.numpy as jnp
        import numpy as np
        N = 6250
        E = 100000
        D = 96
        ED = 17
        src, dst = (edge_index[0], edge_index[1])
        h = jax.nn.relu(edge_attr @ W1.T + b1)
        w = h @ W2.T + b2
        msg = w * x[src]
        agg = jax.ops.segment_sum(msg, dst, num_segments=x.shape[0])
        return jax.nn.relu(x @ Ws.T + bs + agg @ Wn.T + bn)
    edge_index = jnp.stack([src, dst])
    x = _layernorm(x + _L0_gnn_ref(x, edge_index, edge_attr_32, L0_gnn_We, L0_gnn_be, L0_gnn_W1, L0_gnn_b1, L0_gnn_W2, L0_gnn_b2, L0_gnn_gamma, L0_gnn_beta), axis=-1)
    x = _layernorm(x + _L1_gnn_ref(x, edge_index, edge_attr_17, L1_gnn_W1, L1_gnn_b1, L1_gnn_W2, L1_gnn_b2, L1_gnn_Ws, L1_gnn_bs, L1_gnn_Wn, L1_gnn_bn), axis=-1)
    return x

_drawn_inputs = setup_inputs


def setup_inputs(seed=0):
    import zlib

    import numpy as np

    out = dict(_drawn_inputs(seed))
    spreads = {'L0_gnn_be': (0.0, 0.1),
     'L0_gnn_b1': (0.0, 0.8),
     'L0_gnn_b2': (0.0, 0.8),
     'L0_gnn_gamma': (1.0, 0.2),
     'L0_gnn_beta': (0.0, 0.1)}
    factors = {}
    for name, (base, spread) in spreads.items():
        noise = np.random.default_rng([zlib.crc32(name.encode()), seed]).standard_normal(out[name].shape)
        drawn = base * np.exp(spread * noise) if base else spread * noise
        out[name] = jnp.asarray(drawn.astype(out[name].dtype))
    for name, factor in factors.items():
        out[name] = (out[name] * factor).astype(out[name].dtype)
    return out
```

```python
import concourse.bass as bass
from concourse import mybir
from contextlib import ExitStack


def gnn_two_layers_kernel(
    nc: bass.Bass,
    x: bass.AP,
    src: bass.AP,
    dst: bass.AP,
    edge_attr_17: bass.AP,
    edge_attr_32: bass.AP,
    We: bass.AP,
    be: bass.AP,
    W1: bass.AP,
    b1: bass.AP,
    W2: bass.AP,
    b2: bass.AP,
    gamma: bass.AP,
    beta: bass.AP,
    V1T: bass.AP,
    c1: bass.AP,
    V2T: bass.AP,
    c2: bass.AP,
    WsT: bass.AP,
    bs: bass.AP,
    WnT: bass.AP,
    bn: bass.AP,
    out: bass.AP,
):
    f32 = mybir.dt.float32
    i32 = mybir.dt.int32
    u32 = mybir.dt.uint32
    ALU = mybir.AluOpType
    ACT = mybir.ActivationFunctionType
    AX = mybir.AxisListType
    ds = bass.ds

    P = 128
    N, D = x.shape
    E, F0 = edge_attr_32.shape
    F1 = edge_attr_17.shape[1]
    TILES = 8
    HALF = TILES // 2
    BLOCK = P * TILES
    BLOCKS = -(-E // BLOCK)
    RING = 4
    ROUNDS = BLOCKS // RING
    assert ROUNDS * RING == BLOCKS
    WINDOW = 96
    SHARED = (BLOCKS * BLOCK - E) // TILES
    EPS = 1e-5

    KN = 4
    PN = 125
    CHUNK = KN * PN
    CHUNKS = N // CHUNK
    CHUNK_ROUNDS = CHUNKS // RING
    assert CHUNKS * CHUNK == N and CHUNKS == CHUNK_ROUNDS * RING + 1
    SPLIT = 112
    BLK_A = P
    BLK_B = BLOCKS - BLK_A

    ea_rows = [edge_attr_32.rearrange("(r j) f -> r (j f)", j=TILES),
               edge_attr_17.rearrange("(r j) f -> r (j f)", j=TILES)]
    EA_LAST = E // TILES - P
    x1 = nc.dram_tensor("x1_rows", (N, D), f32).ap()

    def rows_of(table):
        return table.rearrange("(q k) f -> q (k f)", k=KN)

    ctx = ExitStack()
    with ctx:
        def sb(name, shape, dt=f32):
            return ctx.enter_context(nc.sbuf_tensor(name, shape, dt))

        def sem(name):
            return ctx.enter_context(nc.semaphore(name))

        ident = sb("ident", [P, P])
        ones = sb("ones", [P, P])
        iota_row = sb("iota_row", [P, WINDOW])
        We_diag = sb("We_diag", [P, HALF * D])
        be_row = sb("be_row", [P, HALF * D])
        pick0 = sb("pick0", [P, P])
        W1_s = sb("W1_s", [D, D])
        W2_s = sb("W2_s", [D, D])
        V1_pad = sb("V1_pad", [HALF * F1, HALF, D])
        V2_s = sb("V2_s", [D + 1, D])
        Ws_s = sb("Ws_s", [D, D])
        Wn_s = sb("Wn_s", [D, D])
        cols = sb("cols", [D, 8])
        b1_c, b2_c, gamma_c, beta_c, c1_c, bs_c, bn_c = (cols[:, n:n + 1] for n in range(7))
        eps_c = sb("eps_c", [P, 1])
        bias_out = sb("bias_out", [D, 1])
        scale_bn = sb("scale_bn", [D, 1])
        shift_bn = sb("shift_bn", [D, 1])
        bn_tmp = sb("bn_tmp", [D, 2])

        srcA = sb("srcA", [BLK_A, BLOCK], i32)
        srcB = sb("srcB", [BLK_B, BLOCK], i32)
        dstA = sb("dstA", [BLK_A, BLOCK], i32)
        dstB = sb("dstB", [BLK_B, BLOCK], i32)
        rowsf = sb("rowsf", [P, 4, BLOCK])
        reach = sb("reach", [P, 2, 2])
        reach_i = sb("reach_i", [P, 2, 2], i32)
        meta = sb("meta", [1, 2 * BLOCKS], i32)
        diag_lo = sb("diag_lo", [P, 2, P])
        lo_all = sb("lo_all", [P, BLOCKS])
        src_all = sb("src_all", [P, (BLOCKS + RING) * TILES], i32)
        rel_all = sb("rel_all", [P, BLOCKS * TILES])

        aggA = sb("aggA", [D, N + WINDOW])
        aggB = sb("aggB", [D, N + WINDOW])

        idx = sb("idx", [P, RING, TILES], i32)
        g = sb("g", [P, RING, TILES * D])
        ea = sb("ea", [P, RING, TILES * F0])
        eaT = sb("eaT", [P, 2, 2 * P])
        hT = sb("hT", [D + 1, BLOCK])
        rel = sb("rel", [P, TILES])
        rel_far = sb("rel_far", [P, TILES])
        onehot = sb("onehot", [P, TILES, WINDOW])

        xr = sb("xr", [PN, RING, KN * D])
        hid = sb("hid", [D, 2, CHUNK])
        bnst = sb("bnst", [D, CHUNKS * 6])
        bnmv = sb("bnmv", [D, 2])
        z = sb("z", [D, 2, KN * PN])
        y = sb("y", [PN, 2, KN * D])
        yn = sb("yn", [PN, 2, KN * D])
        lnst = sb("lnst", [PN, 2, KN * 6])
        lnmv = sb("lnmv", [PN, 2, KN, 2])
        lnsd = sb("lnsd", [PN, 2, KN])
        lnrs = sb("lnrs", [PN, 2, KN])
        lnnb = sb("lnnb", [PN, 2, KN])

        bank = [ctx.enter_context(nc.psum_tensor(f"bank{n}", [P, 512], f32)) for n in range(8)]
        ps_eaT = bank[0:2]
        ps_xT = bank[0:2]
        ps_feat = bank[2:4]
        ps_h = bank[4:6]
        ps_agg = bank[6]
        ps_hid, ps_h2 = bank[0:2], bank[2:4]
        ps_row = bank[4:6]

        idx_rows_in = [sem(f"idx_rows_in{n}") for n in range(4)]
        weights_in = sem("weights_in")
        meta_in = sem("meta_in")
        consts_set = sem("consts_set")
        pads_set = sem("pads_set")
        tables_zeroed = sem("tables_zeroed")
        rows_cast = sem("rows_cast")
        reach_set = sem("reach_set")
        diag_set = sem("diag_set")
        idx_turned = sem("idx_turned")
        idx_taken = sem("idx_taken")
        bias_set = sem("bias_set")
        pool_waited = sem("pool_waited")
        dve_waited = sem("dve_waited")
        ea_in = [sem(f"ea_in{n}") for n in range(RING)]
        rows_in = [sem(f"rows_in{n}") for n in range(RING)]
        idx_ready = sem("idx_ready")
        eaT_made = sem("eaT_made")
        eaT_ready = sem("eaT_ready")
        h_made = sem("h_made")
        hT_ready = sem("hT_ready")
        feat_made = sem("feat_made")
        joined = sem("joined")
        msg_ready = sem("msg_ready")
        rel_set = sem("rel_set")
        onehot_ready = sem("onehot_ready")
        agg_made = sem("agg_made")
        agg_added = sem("agg_added")
        far_rel_set = sem("far_rel_set")
        far_onehot = sem("far_onehot")
        far_made = sem("far_made")
        far_added = sem("far_added")
        xr_in = [sem(f"xr_in{n}") for n in range(RING)]
        xT_made = sem("xT_made")
        xT_ready = sem("xT_ready")
        hid_made = sem("hid_made")
        hid_ready = sem("hid_ready")
        h2_made = sem("h2_made")
        h2_ready = sem("h2_ready")
        stats_ready = sem("stats_ready")
        bn_step = sem("bn_step")
        mix_made = sem("mix_made")
        z_ready = sem("z_ready")
        row_made = sem("row_made")
        y_ready = sem("y_ready")
        lnst_ready = sem("lnst_ready")
        lnmv_ready = sem("lnmv_ready")
        lnsd_ready = sem("lnsd_ready")
        lnrs_ready = sem("lnrs_ready")
        lnnb_ready = sem("lnnb_ready")
        yn_ready = sem("yn_ready")
        stored = [sem(f"stored{n}") for n in range(2)]

        WEIGHT_DMAS = 3 * HALF + 4 + 2 + 7
        STORES = [32 * (CHUNKS // 2 + 1), 32 * (CHUNKS // 2)]
        IDX_GROUPS = [(n, j0) for n in range(4) for j0 in (0, HALF)]

        def each_block(eng, layer, body, at_round=None):
            with eng.Fori(0, ROUNDS) as t:
                facts = at_round(t) if at_round else None
                for u in range(RING):
                    body(t * RING + u, u, t * RING + (u + layer * BLOCKS), t + layer * ROUNDS, facts)

        def each_chunk(eng, body):
            for u in range(RING):
                body(u, u)
            with eng.Fori(1, CHUNK_ROUNDS) as t:
                for u in range(RING):
                    body(t * RING + u, u)
            body(CHUNKS - 1, 0)

        def first(c):
            return isinstance(c, int) and c < 2

        def chunk_reuse(eng, semaphore, c, phase):
            if not first(c):
                eng.wait_ge(semaphore, c + (phase * CHUNKS - 1))
            elif phase:
                eng.wait_ge(semaphore, phase * CHUNKS)

        def xr_wait(eng, c, u, use):
            before = use * (CHUNK_ROUNDS + (u == 0))
            if isinstance(c, int):
                eng.wait_ge(xr_in[u], 32 * (c // RING + 1 + before))
            else:
                eng.wait_ge(xr_in[u], (c - u) * (32 // RING) + 32 * (1 + before))

        def reach_regs(eng):
            regs = [eng.alloc_register(f"reach{n}") for n in range(2 * RING)]

            def at_round(t):
                eng.load(regs, meta[0:1, ds(t * (2 * RING), 2 * RING)])
                vals = [eng.snap(r, min_val=0, max_val=N - 1) for r in regs]
                return [(vals[2 * u], vals[2 * u + 1]) for u in range(RING)]
            return at_round

        block = ctx.enter_context(nc.Block())

        @block.sync
        def _(sp):
            def load_chunk(rows, c, u):
                sp.dma_start(xr[0:SPLIT, u, :], rows[ds(c * PN, SPLIT), :]).then_inc(xr_in[u], 16)
                sp.dma_start(xr[SPLIT:PN, u, :], rows[ds(c * PN + SPLIT, PN - SPLIT), :]).then_inc(xr_in[u], 16)

            def load_to_turn(table, phase):
                rows = rows_of(table)

                def body(c, u):
                    if not (isinstance(c, int) and c < RING):
                        sp.wait_ge(xT_made, c + (phase * CHUNKS - RING + 1))
                    elif phase:
                        sp.wait_ge(y_ready, phase * CHUNKS)
                    load_chunk(rows, c, u)
                each_chunk(sp, body)

            def load_to_add_and_store(table, target, phase):
                rows, to = rows_of(table), rows_of(target)

                def load(c, u):
                    sp.wait_ge(y_ready, c + (phase * CHUNKS - RING + 1))
                    load_chunk(rows, c, u)

                def store(c, u):
                    v = u % 2
                    sp.wait_ge(yn_ready, c + (phase * CHUNKS + 1))
                    sp.dma_start(to[ds(c * PN, SPLIT), :], yn[0:SPLIT, v, :]).then_inc(stored[v], 16)
                    sp.dma_start(to[ds(c * PN + SPLIT, PN - SPLIT), :], yn[SPLIT:PN, v, :]).then_inc(stored[v], 16)

                sp.wait_ge(xT_made, (phase + 1) * CHUNKS)
                for c in range(RING):
                    load_chunk(rows, c, c)
                with sp.Fori(0, CHUNK_ROUNDS - 1) as t:
                    for u in range(RING):
                        store(t * RING + u, u)
                        load(t * RING + (u + RING), u)
                for c in range(CHUNKS - RING - 1, CHUNKS):
                    store(c, c % RING)
                    if c + RING < CHUNKS:
                        load(c + RING, (c + RING) % RING)

            def load_edges(layer, F):
                def load(start, u, s):
                    sp.wait_ge(eaT_made, s + 1)
                    sp.dma_start(ea[:, u, 0:TILES * F], ea_rows[layer][ds(start, P), :]).then_inc(ea_in[u], 16)
                with sp.Fori(0, ROUNDS - 1) as t:
                    for u in range(RING):
                        load(t * (RING * P) + u * P, u, t * RING + (u + layer * BLOCKS))
                for u in range(RING):
                    b = BLOCKS - RING + u
                    load(EA_LAST if b == BLOCKS - 1 else b * P, u, b + layer * BLOCKS)

            full = (BLOCKS - 1 - BLK_A) // 16 * 16
            for n, (a, tA, tB) in enumerate([(src, srcA, srcB), (dst, dstA, dstB)]):
                v = a[0:(BLOCKS - 1) * BLOCK].rearrange("(b e) -> b e", e=BLOCK)
                sp.dma_start(tA[:, :], v[0:BLK_A, :]).then_inc(idx_rows_in[2 * n], 16)
                sp.dma_start(tB[0:full, :], v[BLK_A:BLK_A + full, :]).then_inc(idx_rows_in[2 * n + 1], 16)
                sp.dma_start(tB[full:BLK_B - 1, :], v[BLK_A + full:BLOCKS - 1, :]).then_inc(idx_rows_in[2 * n + 1], 16)
                sp.dma_start(tB[BLK_B - 1:BLK_B, :],
                             a[E - BLOCK:E].rearrange("(b e) -> b e", e=BLOCK)).then_inc(idx_rows_in[2 * n + 1], 16)
            sp.wait_ge(pads_set, 3)
            for k in range(HALF):
                sp.dma_start(We_diag[k * F0:(k + 1) * F0, k * D:(k + 1) * D], We[:, :]).then_inc(weights_in, 16)
                sp.dma_start(be_row[0:1, k * D:(k + 1) * D], be.rearrange("(o d) -> o d", o=1)).then_inc(weights_in, 16)
                sp.dma_start(V1_pad[k * F1:(k + 1) * F1, k, :], V1T[:, :]).then_inc(weights_in, 16)
            for tile, w in ((W1_s, W1), (W2_s, W2), (Ws_s, WsT), (Wn_s, WnT)):
                sp.dma_start(tile[:, :], w[:, :]).then_inc(weights_in, 16)
            sp.dma_start(V2_s[0:D, :], V2T[:, :]).then_inc(weights_in, 16)
            sp.dma_start(V2_s[D:D + 1, :], c2.rearrange("(o d) -> o d", o=1)).then_inc(weights_in, 16)
            for tile, w in ((b1_c, b1), (b2_c, b2), (gamma_c, gamma), (beta_c, beta), (c1_c, c1), (bs_c, bs), (bn_c, bn)):
                sp.dma_start(tile, w.rearrange("(d o) -> d o", o=1)).then_inc(weights_in, 16)
            sp.wait_ge(reach_set, 6)
            sp.dma_start(meta[0:1, 0:2 * BLK_A].rearrange("o (b t) -> o b t", t=2),
                         reach_i[0:BLK_A, 0, :]).then_inc(meta_in, 16)
            sp.dma_start(meta[0:1, 2 * BLK_A:].rearrange("o (b t) -> o b t", t=2),
                         reach_i[0:BLK_B, 1, :]).then_inc(meta_in, 16)

            load_to_turn(x, 0)
            load_edges(0, F0)
            load_to_add_and_store(x, x1, 0)
            for v in range(2):
                sp.wait_ge(stored[v], STORES[v])
            load_to_turn(x1, 1)
            load_edges(1, F1)
            load_to_add_and_store(x1, out, 1)
            for v in range(2):
                sp.wait_ge(stored[v], 2 * STORES[v])

        @block.gpsimd
        def _(pool):
            nc.gpsimd.memset(ident[:, :], 0.0).then_inc(consts_set, 1)
            pool.wait_ge(consts_set, 1)
            nc.gpsimd.affine_select(out=ident[:, :], in_=ident[:, :], compare_op=ALU.not_equal, fill=1.0,
                                    base=0, pattern=[[-1, P]], channel_multiplier=1).then_inc(consts_set, 1)
            nc.gpsimd.memset(We_diag[:, :], 0.0).then_inc(pads_set, 1)
            nc.gpsimd.memset(be_row[:, :], 0.0).then_inc(pads_set, 1)
            nc.gpsimd.memset(V1_pad[:, :, :], 0.0).then_inc(pads_set, 1)
            nc.gpsimd.iota(iota_row[:, :], pattern=[[1, WINDOW]], base=0, channel_multiplier=0,
                           allow_small_or_imprecise_dtypes=True).then_inc(consts_set, 1)
            nc.gpsimd.memset(ones[:, :], 1.0).then_inc(consts_set, 1)
            nc.gpsimd.memset(pick0[:, :], 0.0).then_inc(consts_set, 1)
            pool.wait_ge(consts_set, 5)
            nc.gpsimd.memset(pick0[0:1, :], 1.0).then_inc(consts_set, 1)
            pool.wait_ge(consts_set, 6)
            nc.gpsimd.memset(hT[D:D + 1, :], 1.0).then_inc(consts_set, 1)
            pool.wait_ge(consts_set, 7)
            nc.gpsimd.memset(eps_c[:, :], EPS).then_inc(consts_set, 1)

            def gather(layer, table):
                def body(b, u, s, uses, _):
                    pool.wait_ge(idx_ready, s + 1)
                    pool.wait_ge(agg_made, s + 1)
                    pool.sem_inc(pool_waited, 1)
                    for j in range(TILES):
                        nc.gpsimd.indirect_dma_start(
                            out=g[:, u, j * D:(j + 1) * D], out_offset=None, in_=table[:, :],
                            in_offset=bass.IndirectOffsetOnAxis(ap=idx[:, u, j:j + 1].bitcast(u32), axis=0),
                        ).then_inc(rows_in[u], 16)
                each_block(pool, layer, body)

            def normalize(phase):
                def body(c, u):
                    v = u % 2
                    pool.wait_ge(lnnb_ready, c + (phase * CHUNKS + 1))
                    if not first(c):
                        if isinstance(c, int):
                            pool.wait_ge(stored[v], 32 * (c // 2) + phase * STORES[v])
                        else:
                            pool.wait_ge(stored[v], (c - v) * 16 + phase * STORES[v])
                    elif phase:
                        pool.wait_ge(stored[v], phase * STORES[v])
                    pool.sem_inc(pool_waited, 1)
                    for k in range(KN):
                        last = nc.gpsimd.tensor_scalar(yn[:, v, k * D:(k + 1) * D], y[:, v, k * D:(k + 1) * D],
                                                       lnrs[:, v, k:k + 1], lnnb[:, v, k:k + 1], ALU.mult, ALU.add)
                    last.then_inc(yn_ready, 1)
                each_chunk(pool, body)

            gather(0, x)
            normalize(0)
            for v in range(2):
                pool.wait_ge(stored[v], STORES[v])
            gather(1, x1)
            normalize(1)

        @block.tensor
        def _(pe):
            for q in (eaT_made, eaT_ready, h_made, hT_ready, feat_made, joined, msg_ready, rel_set,
                      onehot_ready, agg_made, agg_added):
                pe.sem_inc(q, RING)

            pe.wait_ge(consts_set, 2)
            for q, (n, j0) in enumerate(IDX_GROUPS):
                nb = BLK_B if n % 2 else BLK_A
                pe.wait_ge(rows_cast, n + 1)
                if q >= 6:
                    pe.wait_ge(idx_taken, q - 5)
                for k in range(HALF):
                    last = nc.tensor.transpose(bank[2 + q % 6][:, k * P:k * P + nb],
                                               rowsf[0:nb, n, :].rearrange("b (p j) -> b j p", j=TILES)[:, j0 + k, :],
                                               ident[0:nb, 0:nb])
                last.then_inc(idx_turned, 1)
            pe.wait_ge(diag_set, 2)
            pe.wait_ge(consts_set, 8)
            pe.wait_ge(idx_taken, 3)
            nc.tensor.matmul(bank[4][:, 0:BLK_A], ones[:, :], diag_lo[:, 0, :], start=True, stop=True)
            nc.tensor.matmul(bank[4][:, BLK_A:BLOCKS], ones[0:BLK_B, :], diag_lo[0:BLK_B, 1, 0:BLK_B],
                             start=True, stop=True).then_inc(idx_turned, 1)

            def turn_rows(phase):
                def body(c, u):
                    v = u % 2
                    xr_wait(pe, c, u, 2 * phase)
                    chunk_reuse(pe, xT_ready, c, phase)
                    for k in range(KN):
                        last = nc.tensor.transpose(ps_xT[v][0:D, k * PN:(k + 1) * PN],
                                                   xr[:, u, k * D:(k + 1) * D], ident[0:PN, 0:PN])
                    last.then_inc(xT_made, 1)
                each_chunk(pe, body)

            turn_rows(0)
            pe.wait_ge(weights_in, 16 * WEIGHT_DMAS)
            pe.wait_ge(meta_in, 32)
            pe.wait_ge(idx_taken, 2 * len(IDX_GROUPS) // 2 + 1)
            pe.wait_ge(xT_ready, CHUNKS)
            at_round = reach_regs(pe)
            far_count = pe.alloc_register("far_count")
            pe.reg_mov(far_count, 0)

            def turn_edges(u, s, uses, F):
                pe.wait_ge(ea_in[u], uses * 16 + 16)
                pe.wait_ge(eaT_ready, s + (RING - 1))
                rows = HALF * F
                for h in range(2):
                    last = nc.tensor.transpose(ps_eaT[u % 2][0:rows, h * P:(h + 1) * P],
                                               ea[:, u, h * rows:(h + 1) * rows], ident[:, :])
                last.then_inc(eaT_made, 1)

            def aggregate(u, s, lo, hi):
                def window():
                    for j in range(TILES):
                        last = nc.tensor.matmul(ps_agg[0:D, 0:WINDOW], g[:, u, j * D:(j + 1) * D], onehot[:, j, :],
                                                start=(j == 0), stop=(j == TILES - 1))
                    return last
                with pe.If(hi >= lo + WINDOW):
                    with pe.Fori(lo + WINDOW, hi + 1, WINDOW) as w:
                        pe.reg_add(far_count, far_count, 1)
                        pe.wait_ge(far_onehot, pe.snap(far_count, min_val=1))
                        window().then_inc(far_made, 1)
                pe.wait_ge(onehot_ready, s + (RING + 1))
                window().then_inc(agg_made, 1)

            def edges0(b, u, s, uses, reach_of):
                turn_edges(u, s, uses, F0)
                pe.wait_ge(eaT_ready, s + (RING + 1))
                for h in range(2):
                    pe.wait_ge(joined, s * 2 + (RING + h - 1))
                    nc.tensor.matmul(ps_feat[h][:, 0:HALF * D], pick0[:, :], be_row[:, :], start=True, stop=False)
                    nc.tensor.matmul(ps_feat[h][:, 0:HALF * D], eaT[:, u % 2, h * P:(h + 1) * P], We_diag[:, :],
                                     start=False, stop=True).then_inc(feat_made, 1)
                pe.wait_ge(msg_ready, s + (RING + 1))
                aggregate(u, s, *reach_of[u])

            def edges1(b, u, s, uses, reach_of):
                turn_edges(u, s, uses, F1)
                pe.wait_ge(eaT_ready, s + (RING + 1))
                for h in range(2):
                    pe.wait_ge(hT_ready, b * 2 + (RING + h - 1))
                    for k in range(HALF):
                        last = nc.tensor.matmul(ps_h[h][0:D, k * P:(k + 1) * P], V1_pad[:, k, :],
                                                eaT[0:HALF * F1, u % 2, h * P:(h + 1) * P], start=True, stop=True)
                    last.then_inc(h_made, 1)
                for h in range(2):
                    pe.wait_ge(hT_ready, b * 2 + (RING + h + 1))
                    pe.wait_ge(joined, s * 2 + (RING + h - 1))
                    for k in range(HALF):
                        j = h * HALF + k
                        last = nc.tensor.matmul(ps_feat[h][:, k * D:(k + 1) * D], hT[:, j * P:(j + 1) * P], V2_s[:, :],
                                                start=True, stop=True)
                    last.then_inc(feat_made, 1)
                pe.wait_ge(joined, s * 2 + (RING + 2))
                aggregate(u, s, *reach_of[u])

            each_block(pe, 0, edges0, at_round)

            pe.wait_ge(agg_added, RING + BLOCKS)

            def second(c, v):
                pe.wait_ge(hid_ready, c + 1)
                if not first(c):
                    pe.wait_ge(h2_ready, c - 1)
                nc.tensor.matmul(ps_h2[v][0:D, 0:CHUNK], W2_s[:, :], hid[:, v, :], start=True, stop=True).then_inc(h2_made, 1)

            def mlp(c, u):
                v = u % 2
                chunk_reuse(pe, hid_ready, c, 0)
                nc.tensor.matmul(ps_hid[v][0:D, 0:CHUNK], W1_s[:, :], aggA[:, ds(c * CHUNK, CHUNK)],
                                 start=True, stop=True).then_inc(hid_made, 1)
                if not (isinstance(c, int) and c == 0):
                    second(c - 1, 1 - v)
            each_chunk(pe, mlp)
            second(CHUNKS - 1, 0)

            def turn_back(c, u, phase):
                v = u % 2
                pe.wait_ge(z_ready, c + (phase * CHUNKS + 1))
                chunk_reuse(pe, y_ready, c, phase)
                for k in range(KN):
                    last = nc.tensor.transpose(ps_row[v][0:PN, k * D:(k + 1) * D], z[:, v, k * PN:(k + 1) * PN],
                                               ident[0:D, 0:D])
                last.then_inc(row_made, 1)

            each_chunk(pe, lambda c, u: turn_back(c, u, 0))

            turn_rows(1)
            pe.wait_ge(xT_ready, 2 * CHUNKS)
            each_block(pe, 1, edges1, at_round)
            pe.wait_ge(agg_added, RING + 2 * BLOCKS)

            def mix(c, u):
                v = u % 2
                if not first(c):
                    pe.wait_ge(z_ready, c + (CHUNKS - 1))
                cols_ = ds(c * CHUNK, CHUNK)
                nc.tensor.matmul(ps_h2[v][0:D, 0:CHUNK], Wn_s[:, :], aggB[:, cols_], start=True, stop=False)
                nc.tensor.matmul(ps_h2[v][0:D, 0:CHUNK], Ws_s[:, :], aggA[:, cols_], start=False, stop=True).then_inc(mix_made, 1)
                if not (isinstance(c, int) and c == 0):
                    turn_back(c - 1, (u - 1) % RING, 1)
            each_chunk(pe, mix)
            turn_back(CHUNKS - 1, 0, 1)

        @block.scalar
        def _(act):
            def turn_rows(phase):
                def body(c, u):
                    act.wait_ge(xT_made, c + (phase * CHUNKS + 1))
                    nc.scalar.copy(aggA[:, ds(c * CHUNK, CHUNK)].rearrange("d (p k) -> d k p", k=KN),
                                   ps_xT[u % 2][0:D, 0:CHUNK].rearrange("d (k p) -> d k p", k=KN)).then_inc(xT_ready, 1)
                each_chunk(act, body)

            def edge_features(u, s, rows, read_by, read_count):
                act.wait_ge(eaT_made, s + (RING + 1))
                act.wait_ge(read_by, read_count)
                nc.scalar.copy(eaT[0:rows, u % 2, :], ps_eaT[u % 2][0:rows, 0:2 * P]).then_inc(eaT_ready, 1)

            def edges0(b, u, s, uses, _):
                edge_features(u, s, HALF * F0, feat_made, s * 2 + (RING - 2))
                act.wait_ge(joined, s * 2 + (RING + 2))
                nc.scalar.activation(g[:, u, :], g[:, u, :], ACT.Relu).then_inc(msg_ready, 1)

            def edges1(b, u, s, uses, _):
                edge_features(u, s, HALF * F1, h_made, b * 2 + (RING - 2))
                for h in range(2):
                    act.wait_ge(h_made, b * 2 + (RING + h + 1))
                    act.wait_ge(feat_made, s * 2 + (RING + h - 1))
                    nc.scalar.activation(hT[0:D, h * HALF * P:(h + 1) * HALF * P], ps_h[h][0:D, :], ACT.Relu,
                                         bias=c1_c).then_inc(hT_ready, 1)

            def normalize_roots(c, v, phase):
                act.wait_ge(lnmv_ready, c + (phase * CHUNKS + 1))
                nc.scalar.activation(lnsd[:, v, :], lnmv[:, v, :, 1], ACT.Sqrt, bias=eps_c[0:PN, :]).then_inc(lnsd_ready, 1)

            act.wait_ge(consts_set, 8)
            turn_rows(0)
            act.wait_ge(weights_in, 16 * WEIGHT_DMAS)
            each_block(act, 0, edges0)

            def mlp(c, u):
                v = u % 2
                act.wait_ge(hid_made, c + 1)
                if not first(c):
                    act.wait_ge(h2_made, c - 1)
                nc.scalar.activation(hid[:, v, :], ps_hid[v][0:D, 0:CHUNK], ACT.Relu, bias=b1_c).then_inc(hid_ready, 1)
            each_chunk(act, mlp)
            act.wait_ge(bn_step, 1)
            nc.scalar.activation(bn_tmp[:, 0:1], bnmv[:, 1:2], ACT.Sqrt, bias=eps_c[0:D, :]).then_inc(bn_step, 1)
            act.wait_ge(bn_step, 6)

            def rows0(c, u):
                v = u % 2
                chunk_reuse(act, row_made, c, 0)
                nc.scalar.activation(z[:, v, :].rearrange("d (k p) -> d k p", k=KN),
                                     aggA[:, ds(c * CHUNK, CHUNK)].rearrange("d (p k) -> d k p", k=KN),
                                     ACT.Relu, bias=shift_bn[:, :], scale=scale_bn[:, :]).then_inc(z_ready, 1)
                if not (isinstance(c, int) and c == 0):
                    normalize_roots(c - 1, 1 - v, 0)
            each_chunk(act, rows0)
            normalize_roots(CHUNKS - 1, 0, 0)

            turn_rows(1)
            each_block(act, 1, edges1)

            def rows1(c, u):
                v = u % 2
                act.wait_ge(mix_made, c + 1)
                chunk_reuse(act, row_made, c, 1)
                nc.scalar.activation(z[:, v, :].rearrange("d (k p) -> d k p", k=KN),
                                     ps_h2[v][0:D, 0:CHUNK].rearrange("d (p k) -> d k p", k=KN),
                                     ACT.Relu, bias=bias_out[:, :]).then_inc(z_ready, 1)
                if not (isinstance(c, int) and c == 0):
                    normalize_roots(c - 1, 1 - v, 1)
            each_chunk(act, rows1)
            normalize_roots(CHUNKS - 1, 0, 1)

        @block.vector
        def _(dve):
            src_v = src_all[:, :].rearrange("p (b j) -> p b j", j=TILES)
            rel_v = rel_all[:, :].rearrange("p (b j) -> p b j", j=TILES)
            raw = [srcA, srcB, dstA, dstB]
            for n in range(4):
                nb = BLK_B if n % 2 else BLK_A
                dve.wait_ge(idx_rows_in[n], 48 if n % 2 else 16)
                nc.vector.tensor_copy(rowsf[0:nb, n, :], raw[n][:, :]).then_inc(rows_cast, 1)
                if n == 1:
                    for q in range(4):
                        m, j0 = IDX_GROUPS[q]
                        b0, nb = (BLK_A, BLK_B) if m % 2 else (0, BLK_A)
                        dve.wait_ge(idx_turned, q + 1)
                        nc.vector.tensor_copy(src_v[:, b0:b0 + nb, j0:j0 + HALF],
                                              bank[2 + q % 6][:, :].rearrange("p (j b) -> p b j", j=HALF)[:, 0:nb, :]
                                              ).then_inc(idx_taken, 1)
                    dve.wait_ge(idx_taken, 4)
                    for u in range(RING):
                        nc.vector.tensor_copy(idx[:, u, :], src_v[:, u, :]).then_inc(idx_ready, 1)
                    nc.vector.tensor_copy(src_v[:, BLOCKS:BLOCKS + RING, :], src_v[:, 0:RING, :]).then_inc(idx_taken, 1)
            for a, nb in ((0, BLK_A), (1, BLK_B)):
                dve.wait_ge(rows_cast, 3 + a)
                for t, op in ((0, ALU.min), (1, ALU.max)):
                    nc.vector.tensor_reduce(reach[0:nb, a, t:t + 1], rowsf[0:nb, 2 + a, :], axis=AX.X, op=op).then_inc(reach_set, 1)
            dve.wait_ge(reach_set, 4)
            dve.wait_ge(consts_set, 2)
            for a, nb in ((0, BLK_A), (1, BLK_B)):
                nc.vector.tensor_copy(reach_i[0:nb, a, :], reach[0:nb, a, :]).then_inc(reach_set, 1)
                nc.vector.tensor_scalar(diag_lo[0:nb, a, 0:nb], ident[0:nb, 0:nb], reach[0:nb, a, 0:1], None,
                                        ALU.mult).then_inc(diag_set, 1)
            dve.wait_ge(idx_turned, len(IDX_GROUPS) + 1)
            nc.vector.tensor_copy(lo_all[:, :], bank[4][:, 0:BLOCKS]).then_inc(diag_set, 1)
            dve.wait_ge(diag_set, 3)
            for q in range(4, 8):
                m, j0 = IDX_GROUPS[q]
                b0, nb = (BLK_A, BLK_B) if m % 2 else (0, BLK_A)
                for k in range(HALF):
                    last = nc.vector.tensor_tensor(rel_v[:, b0:b0 + nb, j0 + k], bank[2 + q % 6][:, k * P:k * P + nb],
                                                   lo_all[:, b0:b0 + nb], ALU.subtract)
                last.then_inc(idx_taken, 1)
            dve.wait_ge(idx_taken, 9)
            nc.vector.memset(rel_v[0:SHARED, BLOCKS - 1, :], -1.0).then_inc(tables_zeroed, 1)
            nc.vector.memset(aggA[:, N:], 0.0).then_inc(tables_zeroed, 1)
            nc.vector.memset(aggB[:, :], 0.0).then_inc(tables_zeroed, 1)
            dve.wait_ge(weights_in, 16 * WEIGHT_DMAS)
            nc.vector.tensor_tensor(bias_out[:, :], bs_c, bn_c, ALU.add).then_inc(bias_set, 1)
            dve.wait_ge(consts_set, 8)
            dve.wait_ge(tables_zeroed, 3)
            dve.wait_ge(meta_in, 32)
            dve.wait_ge(xT_ready, CHUNKS)
            at_round = reach_regs(dve)
            far_count = dve.alloc_register("far_count")
            dve.reg_mov(far_count, 0)

            def edges(layer, op):
                agg = (aggA, aggB)[layer]

                def build_onehot(of):
                    for j in range(TILES):
                        last = nc.vector.tensor_scalar(onehot[:, j, :], iota_row[:, :], of[:, j:j + 1], None, ALU.is_equal)
                    return last

                def add_window(start):
                    return nc.vector.tensor_tensor(agg[:, ds(start, WINDOW)], ps_agg[0:D, 0:WINDOW],
                                                   agg[:, ds(start, WINDOW)], ALU.add)

                def body(b, u, s, uses, reach_of):
                    lo, hi = reach_of[u]
                    nc.vector.tensor_copy(rel[:, :], rel_all[:, ds(b * TILES, TILES)]).then_inc(rel_set, 1)
                    nc.vector.tensor_copy(rel_far[:, :], rel_all[:, ds(b * TILES, TILES)]).then_inc(rel_set, 1)
                    dve.wait_ge(rows_in[u], uses * (16 * TILES) + 16 * TILES)
                    for h in range(2):
                        half = g[:, u, h * HALF * D:(h + 1) * HALF * D]
                        dve.wait_ge(feat_made, s * 2 + (RING + h + 1))
                        nc.vector.tensor_tensor(half, ps_feat[h][:, 0:HALF * D], half, op).then_inc(joined, 1)
                    nc.vector.tensor_copy(idx[:, u, :], src_all[:, ds((b + RING) * TILES, TILES)]).then_inc(idx_ready, 1)
                    dve.wait_ge(rel_set, s * 2 + (RING + 2))
                    with dve.If(hi >= lo + WINDOW):
                        with dve.Fori(lo + WINDOW, hi + 1, WINDOW) as w:
                            dve.reg_add(far_count, far_count, 1)
                            n = dve.snap(far_count, min_val=1)
                            nc.vector.tensor_scalar(rel_far[:, :], rel_far[:, :], -float(WINDOW), None,
                                                    ALU.add).then_inc(far_rel_set, 1)
                            dve.wait_ge(far_rel_set, n)
                            build_onehot(rel_far).then_inc(far_onehot, 1)
                            dve.wait_ge(far_made, n)
                            add_window(w).then_inc(far_added, 1)
                            dve.wait_ge(far_added, n)
                    build_onehot(rel).then_inc(onehot_ready, 1)
                    dve.wait_ge(agg_made, s + (RING + 1))
                    add_window(lo).then_inc(agg_added, 1)
                    dve.wait_ge(agg_added, s + (RING + 1))
                each_block(dve, layer, body, at_round)

            edges(0, ALU.add)

            def mlp(c, u):
                v = u % 2
                chunk = aggA[:, ds(c * CHUNK, CHUNK)]
                dve.wait_ge(h2_made, c + 1)
                nc.vector.tensor_scalar(chunk, ps_h2[v][0:D, 0:CHUNK], b2_c, None, ALU.add).then_inc(h2_ready, 1)
                dve.wait_ge(h2_ready, c + 1)
                nc.vector.bn_stats(bnst[:, ds(c * 6, 6)], chunk).then_inc(stats_ready, 1)
            each_chunk(dve, mlp)
            dve.wait_ge(stats_ready, CHUNKS)
            nc.vector.bn_aggr(bnmv[:, :], bnst[:, :]).then_inc(bn_step, 1)
            dve.wait_ge(bn_step, 2)
            nc.vector.reciprocal(bn_tmp[:, 1:2], bn_tmp[:, 0:1]).then_inc(bn_step, 1)
            dve.wait_ge(bn_step, 3)
            nc.vector.tensor_tensor(scale_bn[:, :], bn_tmp[:, 1:2], gamma_c, ALU.mult).then_inc(bn_step, 1)
            dve.wait_ge(bn_step, 4)
            nc.vector.scalar_tensor_tensor(out=shift_bn[:, :], in0=bnmv[:, 0:1], scalar=-1.0, in1=scale_bn[:, :],
                                           op0=ALU.mult, op1=ALU.mult).then_inc(bn_step, 1)
            dve.wait_ge(bn_step, 5)
            nc.vector.tensor_tensor(shift_bn[:, :], shift_bn[:, :], beta_c, ALU.add).then_inc(bn_step, 1)

            def normalize(phase):
                def stats(c, u):
                    v = u % 2
                    dve.wait_ge(row_made, c + (phase * CHUNKS + 1))
                    xr_wait(dve, c, u, 2 * phase + 1)
                    chunk_reuse(dve, yn_ready, c, phase)
                    nc.vector.tensor_tensor(y[:, v, :], ps_row[v][0:PN, 0:KN * D], xr[:, u, :], ALU.add).then_inc(y_ready, 1)
                    dve.wait_ge(y_ready, c + (phase * CHUNKS + 1))
                    for k in range(KN):
                        last = nc.vector.bn_stats(lnst[:, v, 6 * k:6 * k + 6], y[:, v, k * D:(k + 1) * D])
                    last.then_inc(lnst_ready, 1)
                    dve.wait_ge(lnst_ready, c + (phase * CHUNKS + 1))
                    chunk_reuse(dve, lnsd_ready, c, phase)
                    dve.sem_inc(dve_waited, 1)
                    for k in range(KN):
                        last = nc.vector.bn_aggr(lnmv[:, v, k, :], lnst[:, v, 6 * k:6 * k + 6])
                    last.then_inc(lnmv_ready, 1)

                def factors(c, v):
                    dve.wait_ge(lnsd_ready, c + (phase * CHUNKS + 1))
                    nc.vector.reciprocal(lnrs[:, v, :], lnsd[:, v, :]).then_inc(lnrs_ready, 1)
                    dve.wait_ge(lnrs_ready, c + (phase * CHUNKS + 1))
                    nc.vector.scalar_tensor_tensor(out=lnnb[:, v, :], in0=lnmv[:, v, :, 0], scalar=-1.0, in1=lnrs[:, v, :],
                                                   op0=ALU.mult, op1=ALU.mult).then_inc(lnnb_ready, 1)

                def body(c, u):
                    stats(c, u)
                    if not (isinstance(c, int) and c == 0):
                        factors(c - 1, 1 - u % 2)
                each_chunk(dve, body)
                factors(CHUNKS - 1, 0)

            normalize(0)
            edges(1, ALU.mult)
            normalize(1)


_INS = ['x', 'src', 'dst', 'edge_attr_17', 'edge_attr_32', 'L0_gnn_We', 'L0_gnn_be', 'L0_gnn_W1', 'L0_gnn_b1',
        'L0_gnn_W2', 'L0_gnn_b2', 'L0_gnn_gamma', 'L0_gnn_beta', 'L1_gnn_W1', 'L1_gnn_b1', 'L1_gnn_W2', 'L1_gnn_b2',
        'L1_gnn_Ws', 'L1_gnn_bs', 'L1_gnn_Wn', 'L1_gnn_bn']
_TRANSPOSED = ('L1_gnn_W1', 'L1_gnn_W2', 'L1_gnn_Ws', 'L1_gnn_Wn')
_OUTS = [((12500, 96), 'float32')]


def kernel(**inputs):
    import numpy as _np
    import concourse.bacc as _bacc
    from concourse import mybir as _mybir
    from concourse.bass_utils import run_bass_kernel_spmd as _run

    nc = _bacc.Bacc("TRN2", target_bir_lowering=False, num_devices=1)
    arrays, args = {}, []
    for name in _INS:
        a = _np.asarray(inputs[name])
        a = _np.ascontiguousarray(a.T if name in _TRANSPOSED else a)
        arrays[f"in_{name}_dram"] = a
        args.append(nc.dram_tensor(f"in_{name}_dram", a.shape, _mybir.dt.from_np(a.dtype), kind="ExternalInput").ap())
    for i, (shape, dtype) in enumerate(_OUTS):
        dt = _mybir.dt.from_np(_np.dtype(dtype))
        args.append(nc.dram_tensor(f"out_{i}_dram", shape, dt, kind="ExternalOutput").ap())
    gnn_two_layers_kernel(nc, *args)
    r = _run(nc, [arrays], core_ids=[0])
    got = tuple(r.results[0][f"out_{i}_dram"] for i in range(len(_OUTS)))
    return got[0]
```

```python
import concourse.bass as bass
from concourse import mybir
from contextlib import ExitStack


def gnn_two_layers_kernel(
    nc: bass.Bass,
    x: bass.AP,
    src: bass.AP,
    dst: bass.AP,
    edge_attr_17: bass.AP,
    edge_attr_32: bass.AP,
    We: bass.AP,
    be: bass.AP,
    W1: bass.AP,
    b1: bass.AP,
    W2: bass.AP,
    b2: bass.AP,
    gamma: bass.AP,
    beta: bass.AP,
    V1T: bass.AP,
    c1: bass.AP,
    V2T: bass.AP,
    c2: bass.AP,
    WsT: bass.AP,
    bs: bass.AP,
    WnT: bass.AP,
    bn: bass.AP,
    out: bass.AP,
):
    f32 = mybir.dt.float32
    bf16 = mybir.dt.bfloat16
    i32 = mybir.dt.int32
    u32 = mybir.dt.uint32
    ALU = mybir.AluOpType
    ACT = mybir.ActivationFunctionType
    AX = mybir.AxisListType
    ds = bass.ds

    P = 128
    N, D = x.shape
    E, F0 = edge_attr_32.shape
    F1 = edge_attr_17.shape[1]
    TILES = 8
    HALF = TILES // 2
    BLOCK = P * TILES
    BLOCKS = -(-E // BLOCK)
    RING = 4
    ROUNDS = BLOCKS // RING
    assert ROUNDS * RING == BLOCKS
    WINDOW = 96
    META = 12
    SHARED = (BLOCKS * BLOCK - E) // TILES
    EPS = 1e-5

    KN = 4
    PN = 125
    CHUNK = KN * PN
    CHUNKS = N // CHUNK
    CHUNK_ROUNDS = CHUNKS // RING
    assert CHUNKS * CHUNK == N and CHUNKS == CHUNK_ROUNDS * RING + 1
    SPLIT = 112
    BLK_A = P
    BLK_B = BLOCKS - BLK_A

    ea_rows = [edge_attr_32.rearrange("(r j) f -> r (j f)", j=TILES),
               edge_attr_17.rearrange("(r j) f -> r (j f)", j=TILES)]
    EA_LAST = E // TILES - P
    x1 = nc.dram_tensor("x1_rows", (N, D), f32).ap()

    ctx = ExitStack()
    with ctx:
        def sb(name, shape, dt=f32):
            return ctx.enter_context(nc.sbuf_tensor(name, shape, dt))

        def sem(name):
            return ctx.enter_context(nc.semaphore(name))

        ident = sb("ident", [P, P])
        ones = sb("ones", [P, P])
        iota_row = sb("iota_row", [P, WINDOW])
        We_diag = sb("We_diag", [P, HALF * D])
        be_rows = sb("be_rows", [P, HALF * D], bf16)
        pick3 = sb("pick3", [P, P], bf16)
        be_left = sb("be_left", [3, 3, HALF * D])
        be_part = sb("be_part", [3, 3, HALF * D], bf16)
        W1_s = sb("W1_s", [D, D])
        W2_s = sb("W2_s", [D, D])
        V1_pad = sb("V1_pad", [HALF * F1, HALF, D])
        V2_s = sb("V2_s", [D + 1, D])
        Ws_s = sb("Ws_s", [D, D])
        Wn_s = sb("Wn_s", [D, D])
        cols = sb("cols", [D, 8])
        b1_c, b2_c, gamma_c, beta_c, c1_c, bs_c, bn_c = (cols[:, n:n + 1] for n in range(7))
        eps_c = sb("eps_c", [P, 1])
        bias_out = sb("bias_out", [D, 1])
        scale_bn = sb("scale_bn", [D, 1])
        shift_bn = sb("shift_bn", [D, 1])
        bn_tmp = sb("bn_tmp", [D, 2])

        shared = sb("shared", [P, 4 * BLOCK])
        raw = [shared[0:nb, n * BLOCK:(n + 1) * BLOCK].bitcast(i32)
               for n, nb in enumerate((BLK_A, BLK_B, BLK_A, BLK_B))]
        at = 2 * CHUNK
        z = shared[0:D, 0:at].rearrange("d (v n) -> d v n", v=2)
        y, yn = (shared[0:PN, at + n * 2 * KN * D:at + (n + 1) * 2 * KN * D].rearrange("p (v n) -> p v n", v=2)
                 for n in range(2))
        at += 4 * KN * D
        xr = shared[0:PN, at:at + RING * KN * D].rearrange("p (v n) -> p v n", v=RING)

        rowsf = sb("rowsf", [P, 4, BLOCK])
        reach = sb("reach", [P, 2, 2])
        meta = sb("meta", [1, ROUNDS * META], i32)
        diag = sb("diag", [P, 4, P])
        lo_all = sb("lo_all", [P, BLOCKS])
        least = sb("least", [CHUNKS, 2, ROUNDS])
        chunk_end = sb("chunk_end", [CHUNKS, 1])
        passed = sb("passed", [CHUNKS, ROUNDS])
        src_all = sb("src_all", [P, (BLOCKS + RING) * TILES], i32)
        rel_all = sb("rel_all", [P, BLOCKS * TILES])

        aggA = sb("aggA", [D, N + WINDOW])
        aggB = sb("aggB", [D, N + WINDOW])

        idx = sb("idx", [P, RING, TILES], i32)
        g = sb("g", [P, RING, TILES * D])
        ea = sb("ea", [P, RING, TILES * F0])
        eaT = sb("eaT", [P, 2, 2 * P])
        hT = sb("hT", [D + 1, BLOCK])
        rel = sb("rel", [P, TILES])
        rel_far = sb("rel_far", [P, TILES])
        onehot = sb("onehot", [P, TILES, WINDOW])
        onehot_far = sb("onehot_far", [P, TILES, WINDOW])

        ck_rows = sb("ck_rows", [PN, KN * D])
        ck_in = sb("ck_in", [D, CHUNK])
        ck_mid = sb("ck_mid", [D, CHUNK])
        ck_y = sb("ck_y", [PN, KN * D])
        ck_yn = sb("ck_yn", [PN, KN * D])
        ck_lnst = sb("ck_lnst", [PN, KN * 6])
        ck_lnmv = sb("ck_lnmv", [PN, KN, 2])
        ck_lnsd = sb("ck_lnsd", [PN, KN])
        ck_lnrs = sb("ck_lnrs", [PN, KN])
        ck_lnnb = sb("ck_lnnb", [PN, KN])

        bnst = sb("bnst", [D, CHUNKS * 6])
        bnmv = sb("bnmv", [D, 2])
        lnst = sb("lnst", [PN, 2, KN * 6])
        lnmv = sb("lnmv", [PN, 2, KN, 2])
        lnsd = sb("lnsd", [PN, 2, KN])
        lnrs = sb("lnrs", [PN, 2, KN])
        lnnb = sb("lnnb", [PN, 2, KN])

        bank = [ctx.enter_context(nc.psum_tensor(f"bank{n}", [P, 512], f32)) for n in range(8)]
        ps_eaT = bank[0]
        ps_ck = bank[1]
        ps_ck_mid = bank[7]
        ps_feat = bank[2:4]
        ps_h = bank[4:6]
        ps_agg = bank[6]
        ps_row = bank[4:6]

        idx_rows_in = [sem(f"idx_rows_in{n}") for n in range(4)]
        weights_in = sem("weights_in")
        meta_set = sem("meta_set")
        least_set = sem("least_set")
        be_split = sem("be_split")
        consts_set = sem("consts_set")
        pads_set = sem("pads_set")
        tables_zeroed = sem("tables_zeroed")
        rows_cast = sem("rows_cast")
        reach_set = sem("reach_set")
        diag_set = sem("diag_set")
        idx_turned = sem("idx_turned")
        idx_taken = sem("idx_taken")
        bias_set = sem("bias_set")
        pool_waited = sem("pool_waited")
        dve_waited = sem("dve_waited")
        ea_in = [sem(f"ea_in{n}") for n in range(RING)]
        rows_in = [sem(f"rows_in{n}") for n in range(RING)]
        idx_ready = sem("idx_ready")
        eaT_made = sem("eaT_made")
        eaT_ready = sem("eaT_ready")
        h_made = sem("h_made")
        hT_ready = sem("hT_ready")
        feat_made = sem("feat_made")
        joined = sem("joined")
        msg_ready = sem("msg_ready")
        rel_set = sem("rel_set")
        onehot_ready = sem("onehot_ready")
        agg_made = sem("agg_made")
        agg_added = sem("agg_added")
        far_rel_set = sem("far_rel_set")
        far_onehot = sem("far_onehot")
        far_made = sem("far_made")
        far_added = sem("far_added")
        ck_rows_in = sem("ck_rows_in")
        ck_turned = sem("ck_turned")
        ck_in_ready = sem("ck_in_ready")
        ck_mid_made = sem("ck_mid_made")
        ck_mid_ready = sem("ck_mid_ready")
        ck_out_made = sem("ck_out_made")
        ck_out_ready = sem("ck_out_ready")
        ck_lnst_ready = sem("ck_lnst_ready")
        ck_lnmv_ready = sem("ck_lnmv_ready")
        ck_lnsd_ready = sem("ck_lnsd_ready")
        ck_lnrs_ready = sem("ck_lnrs_ready")
        ck_lnnb_ready = sem("ck_lnnb_ready")
        ck_yn_ready = sem("ck_yn_ready")
        ck_yn_free = sem("ck_yn_free")
        ck_stored = sem("ck_stored")
        xr_in = [sem(f"xr_in{n}") for n in range(RING)]
        stats_ready = sem("stats_ready")
        bn_step = sem("bn_step")
        z_ready = sem("z_ready")
        row_made = sem("row_made")
        y_ready = sem("y_ready")
        lnst_ready = sem("lnst_ready")
        lnmv_ready = sem("lnmv_ready")
        lnsd_ready = sem("lnsd_ready")
        lnrs_ready = sem("lnrs_ready")
        lnnb_ready = sem("lnnb_ready")
        yn_ready = sem("yn_ready")
        stored = [sem(f"stored{n}") for n in range(2)]

        WEIGHT_DMAS = 3 * HALF + 4 + 2 + 7
        STORES = [32 * (CHUNKS // 2 + 1), 32 * (CHUNKS // 2)]
        IDX_GROUPS = [(n, j0) for n in range(4) for j0 in (0, HALF)]
        SHIFTS = [1 << n for n in range((ROUNDS - 1).bit_length())]
        PASSED_SET = 2 * len(SHIFTS) + 2
        META_DUE = 2 * RING

        def each_chunk(eng, body):
            for u in range(RING):
                body(u, u)
            with eng.Fori(1, CHUNK_ROUNDS) as t:
                for u in range(RING):
                    body(t * RING + u, u)
            body(CHUNKS - 1, 0)

        def first(c):
            return isinstance(c, int) and c < 2

        def chunk_reuse(eng, semaphore, c):
            if not first(c):
                eng.wait_ge(semaphore, c - 1)

        class Rounds:

            def __init__(self, eng, name, values):
                self.eng = eng
                self.table = [eng.alloc_register(f"{name}_table{n}") for n in range(values)]
                self.chunk = eng.alloc_register(f"{name}_chunk")
                self.far = eng.alloc_register(f"{name}_far")
                eng.reg_mov(self.far, 0)

            def start_layer(self):
                self.eng.reg_mov(self.chunk, 0)

            def load(self, t, at=0):
                self.eng.load(self.table, meta[0:1, ds(t * META + at, len(self.table))])

            def reach(self, u):
                return (self.eng.snap(self.table[u], min_val=0, max_val=N - 1),
                        self.eng.snap(self.table[RING + u], min_val=0, max_val=N - 1))

            def due(self):
                return self.eng.snap(self.table[-1], min_val=0, max_val=CHUNKS)

            def next_chunk(self):
                return self.eng.snap(self.chunk, min_val=0, max_val=CHUNKS)

            def due_chunk(self):
                return self.eng.snap(self.chunk, min_val=0, max_val=CHUNKS - 1)

            def chunk_done(self):
                self.eng.reg_add(self.chunk, self.chunk, 1)

            def next_far(self):
                self.eng.reg_add(self.far, self.far, 1)
                return self.eng.snap(self.far, min_val=1)

        def chunk_cols(c):
            return ds(c * CHUNK, CHUNK)

        block = ctx.enter_context(nc.Block())

        @block.sync
        def _(sp):
            def rows_of(table):
                return table.rearrange("(q k) f -> q (k f)", k=KN)

            def load_chunk(tile, table, c, semaphore):
                rows = rows_of(table)
                sp.dma_start(tile[0:SPLIT, :], rows[ds(c * PN, SPLIT), :]).then_inc(semaphore, 16)
                sp.dma_start(tile[SPLIT:PN, :], rows[ds(c * PN + SPLIT, PN - SPLIT), :]).then_inc(semaphore, 16)

            def store_chunk(table, c, tile, semaphore):
                rows = rows_of(table)
                sp.dma_start(rows[ds(c * PN, SPLIT), :], tile[0:SPLIT, :]).then_inc(semaphore, 16)
                sp.dma_start(rows[ds(c * PN + SPLIT, PN - SPLIT), :], tile[SPLIT:PN, :]).then_inc(semaphore, 16)

            full = (BLOCKS - 1 - BLK_A) // 16 * 16
            for n, (a, tA, tB) in enumerate([(src, raw[0], raw[1]), (dst, raw[2], raw[3])]):
                v = a[0:(BLOCKS - 1) * BLOCK].rearrange("(b e) -> b e", e=BLOCK)
                sp.dma_start(tA, v[0:BLK_A, :]).then_inc(idx_rows_in[2 * n], 16)
                sp.dma_start(tB[0:full, :], v[BLK_A:BLK_A + full, :]).then_inc(idx_rows_in[2 * n + 1], 16)
                sp.dma_start(tB[full:BLK_B - 1, :], v[BLK_A + full:BLOCKS - 1, :]).then_inc(idx_rows_in[2 * n + 1], 16)
                sp.dma_start(tB[BLK_B - 1:BLK_B, :],
                             a[E - BLOCK:E].rearrange("(b e) -> b e", e=BLOCK)).then_inc(idx_rows_in[2 * n + 1], 16)
            sp.wait_ge(pads_set, 2)
            for k in range(HALF):
                sp.dma_start(We_diag[k * F0:(k + 1) * F0, k * D:(k + 1) * D], We[:, :]).then_inc(weights_in, 16)
                sp.dma_start(be_left[:, 0, k * D:(k + 1) * D],
                             be.rearrange("(o d) -> o d", o=1).to_broadcast([3, D])).then_inc(weights_in, 16)
                sp.dma_start(V1_pad[k * F1:(k + 1) * F1, k, :], V1T[:, :]).then_inc(weights_in, 16)
            for tile, w in ((W1_s, W1), (W2_s, W2), (Ws_s, WsT), (Wn_s, WnT)):
                sp.dma_start(tile[:, :], w[:, :]).then_inc(weights_in, 16)
            sp.dma_start(V2_s[0:D, :], V2T[:, :]).then_inc(weights_in, 16)
            sp.dma_start(V2_s[D:D + 1, :], c2.rearrange("(o d) -> o d", o=1)).then_inc(weights_in, 16)
            for tile, w in ((b1_c, b1), (b2_c, b2), (gamma_c, gamma), (beta_c, beta), (c1_c, c1), (bs_c, bs), (bn_c, bn)):
                sp.dma_start(tile, w.rearrange("(d o) -> d o", o=1)).then_inc(weights_in, 16)

            rounds = Rounds(sp, "sp", 1)
            stores = sp.alloc_register("sp_stores")
            loaded = sp.alloc_register("sp_loaded")

            def edges(layer, F, table):
                rounds.start_layer()
                sp.reg_mov(stores, 0)

                def load_edges(start, u, s):
                    sp.wait_ge(eaT_made, s + 1)
                    sp.dma_start(ea[:, u, 0:TILES * F], ea_rows[layer][ds(start, P), :]).then_inc(ea_in[u], 16)

                def stored_so_far():
                    return sp.snap(stores, min_val=0, max_val=CHUNKS - 1)

                def store(c):
                    sp.wait_ge(ck_yn_ready, c + 1)
                    store_chunk(out, c, ck_yn, ck_stored)
                    sp.wait_ge(ck_stored, c * 32 + 32)
                    sp.sem_inc(ck_yn_free, 1)
                    sp.reg_add(stores, stores, 1)

                def load(c):
                    sp.wait_ge(ck_out_ready, c + (layer * CHUNKS + 1))
                    load_chunk(ck_rows, table, c, ck_rows_in)

                def one_round(t):
                    for u in range(RING):
                        last = isinstance(t, int) and t == ROUNDS - 1 and u == RING - 1
                        load_edges(EA_LAST if last else t * (RING * P) + u * P, u, t * RING + (u + layer * BLOCKS))
                    if layer == 0 and isinstance(t, int) and t == 0:
                        sp.wait_ge(meta_set, 3)
                    rounds.load(t, META_DUE)
                    sp.reg_mov(loaded, rounds.chunk)
                    with sp.If(rounds.due() >= rounds.next_chunk() + 1):
                        load(rounds.due_chunk())
                        rounds.chunk_done()
                    if layer:
                        store_if_behind()

                def store_if_behind():
                    with sp.If(sp.snap(loaded, min_val=0, max_val=CHUNKS) >= sp.snap(stores, min_val=0, max_val=CHUNKS) + 1):
                        store(stored_so_far())

                one_round(0)
                with sp.Fori(1, ROUNDS - 1) as t:
                    one_round(t)
                one_round(ROUNDS - 1)
                if layer:
                    sp.reg_mov(loaded, rounds.chunk)
                    store_if_behind()
                with sp.If(rounds.next_chunk() < CHUNKS):
                    with sp.Fori(rounds.next_chunk(), CHUNKS) as c:
                        load(c)
                        if layer:
                            store(c)

            edges(0, F0, x)

            def load(c, u):
                sp.wait_ge(y_ready, c - (RING - 1))
                load_chunk(xr[:, u, :], x, c, xr_in[u])

            def store(c, u):
                sp.wait_ge(yn_ready, c + 1)
                store_chunk(x1, c, yn[:, u % 2, :], stored[u % 2])

            for c in range(RING):
                load_chunk(xr[:, c, :], x, c, xr_in[c])
            with sp.Fori(0, CHUNK_ROUNDS - 1) as t:
                for u in range(RING):
                    store(t * RING + u, u)
                    load(t * RING + (u + RING), u)
            for c in range(CHUNKS - RING - 1, CHUNKS):
                store(c, c % RING)
                if c + RING < CHUNKS:
                    load(c + RING, (c + RING) % RING)
            for v in range(2):
                sp.wait_ge(stored[v], STORES[v])
            edges(1, F1, x1)
            sp.wait_ge(ck_stored, 32 * CHUNKS)

        @block.gpsimd
        def _(pool):
            nc.gpsimd.memset(ident[:, :], 0.0).then_inc(consts_set, 1)
            pool.wait_ge(consts_set, 1)
            nc.gpsimd.affine_select(out=ident[:, :], in_=ident[:, :], compare_op=ALU.not_equal, fill=1.0,
                                    base=0, pattern=[[-1, P]], channel_multiplier=1).then_inc(consts_set, 1)
            nc.gpsimd.memset(We_diag[:, :], 0.0).then_inc(pads_set, 1)
            nc.gpsimd.memset(V1_pad[:, :, :], 0.0).then_inc(pads_set, 1)
            nc.gpsimd.iota(iota_row[:, :], pattern=[[1, WINDOW]], base=0, channel_multiplier=0,
                           allow_small_or_imprecise_dtypes=True).then_inc(consts_set, 1)
            nc.gpsimd.memset(ones[:, :], 1.0).then_inc(consts_set, 1)
            nc.gpsimd.memset(pick3[:, :], 0.0).then_inc(consts_set, 1)
            nc.gpsimd.memset(be_rows[:, :], 0.0).then_inc(consts_set, 1)
            nc.gpsimd.iota(chunk_end[:, :], pattern=[[0, 1]], base=CHUNK, channel_multiplier=CHUNK,
                           allow_small_or_imprecise_dtypes=True).then_inc(consts_set, 1)
            pool.wait_ge(consts_set, 7)
            nc.gpsimd.memset(pick3[0:3, :], 1.0).then_inc(consts_set, 1)
            pool.wait_ge(consts_set, 8)
            nc.gpsimd.memset(hT[D:D + 1, :], 1.0).then_inc(consts_set, 1)
            pool.wait_ge(consts_set, 9)
            nc.gpsimd.memset(eps_c[:, :], EPS).then_inc(consts_set, 1)

            def gather(layer, table):
                with pool.Fori(0, ROUNDS) as t:
                    for u in range(RING):
                        s = t * RING + (u + layer * BLOCKS)
                        pool.wait_ge(idx_ready, s + 1)
                        pool.wait_ge(agg_made, s + 1)
                        pool.sem_inc(pool_waited, 1)
                        for j in range(TILES):
                            nc.gpsimd.indirect_dma_start(
                                out=g[:, u, j * D:(j + 1) * D], out_offset=None, in_=table[:, :],
                                in_offset=bass.IndirectOffsetOnAxis(ap=idx[:, u, j:j + 1].bitcast(u32), axis=0),
                            ).then_inc(rows_in[u], 16)

            def normalize(c, u):
                v = u % 2
                pool.wait_ge(lnnb_ready, c + 1)
                if not first(c):
                    pool.wait_ge(stored[v], 32 * (c // 2) if isinstance(c, int) else (c - v) * 16)
                pool.sem_inc(pool_waited, 1)
                for k in range(KN):
                    last = nc.gpsimd.tensor_scalar(yn[:, v, k * D:(k + 1) * D], y[:, v, k * D:(k + 1) * D],
                                                   lnrs[:, v, k:k + 1], lnnb[:, v, k:k + 1], ALU.mult, ALU.add)
                last.then_inc(yn_ready, 1)

            gather(0, x)
            each_chunk(pool, normalize)
            for v in range(2):
                pool.wait_ge(stored[v], STORES[v])
            gather(1, x1)

        @block.tensor
        def _(pe):
            for q in (eaT_made, eaT_ready, h_made, hT_ready, feat_made, joined, msg_ready, rel_set,
                      onehot_ready, agg_made, agg_added):
                pe.sem_inc(q, RING)
            for q in (ck_mid_made, ck_mid_ready, ck_out_made, ck_out_ready, ck_yn_free):
                pe.sem_inc(q, 1)

            pe.wait_ge(consts_set, 2)
            for q, (n, j0) in enumerate(IDX_GROUPS):
                nb = BLK_B if n % 2 else BLK_A
                pe.wait_ge(rows_cast, n + 1)
                if q >= 6:
                    pe.wait_ge(idx_taken, q - 5)
                for k in range(HALF):
                    last = nc.tensor.transpose(bank[2 + q % 6][:, k * P:k * P + nb],
                                               rowsf[0:nb, n, :].rearrange("b (p j) -> b j p", j=TILES)[:, j0 + k, :],
                                               ident[0:nb, 0:nb])
                last.then_inc(idx_turned, 1)
            pe.wait_ge(diag_set, 4)
            pe.wait_ge(consts_set, 10)
            pe.wait_ge(idx_taken, 3)
            for t in range(2):
                nc.tensor.matmul(bank[4][:, t * P * 2:t * P * 2 + BLK_A], ones[:, :], diag[:, 2 * t, :], start=True, stop=True)
                last = nc.tensor.matmul(bank[4][:, t * P * 2 + BLK_A:t * P * 2 + BLOCKS], ones[0:BLK_B, :],
                                        diag[0:BLK_B, 2 * t + 1, 0:BLK_B], start=True, stop=True)
            last.then_inc(idx_turned, 1)
            pe.wait_ge(least_set, PASSED_SET)
            nc.tensor.matmul(bank[1][:, 0:ROUNDS], ones[0:CHUNKS, :], passed[:, :], start=True, stop=True).then_inc(idx_turned, 1)
            pe.wait_ge(weights_in, 16 * WEIGHT_DMAS)
            pe.wait_ge(be_split, 9)
            pe.wait_ge(idx_taken, 9)
            pe.wait_ge(meta_set, 3)

            rounds = Rounds(pe, "pe", META_DUE + 1)

            def turn_edges(u, s, uses, F):
                pe.wait_ge(ea_in[u], uses * 16 + 16)
                pe.wait_ge(eaT_ready, s + RING)
                rows = HALF * F
                for h in range(2):
                    last = nc.tensor.transpose(ps_eaT[0:rows, h * P:(h + 1) * P],
                                               ea[:, u, h * rows:(h + 1) * rows], ident[:, :])
                last.then_inc(eaT_made, 1)

            def features0(b, u, s):
                pe.wait_ge(eaT_ready, s + (RING + 1))
                for h in range(2):
                    pe.wait_ge(joined, s * 2 + (RING + h - 1))
                    nc.tensor.matmul(ps_feat[h][:, 0:HALF * D], pick3[:, :], be_rows[:, :], start=True, stop=False)
                    nc.tensor.matmul(ps_feat[h][:, 0:HALF * D], eaT[:, u % 2, h * P:(h + 1) * P], We_diag[:, :],
                                     start=False, stop=True).then_inc(feat_made, 1)

            def features1(b, u, s):
                pe.wait_ge(eaT_ready, s + (RING + 1))
                for h in range(2):
                    pe.wait_ge(hT_ready, b * 2 + (RING + h - 1))
                    for k in range(HALF):
                        last = nc.tensor.matmul(ps_h[h][0:D, k * P:(k + 1) * P], V1_pad[:, k, :],
                                                eaT[0:HALF * F1, u % 2, h * P:(h + 1) * P], start=True, stop=True)
                    last.then_inc(h_made, 1)
                for h in range(2):
                    pe.wait_ge(hT_ready, b * 2 + (RING + h + 1))
                    pe.wait_ge(joined, s * 2 + (RING + h - 1))
                    for k in range(HALF):
                        j = h * HALF + k
                        last = nc.tensor.matmul(ps_feat[h][:, k * D:(k + 1) * D], hT[:, j * P:(j + 1) * P], V2_s[:, :],
                                                start=True, stop=True)
                    last.then_inc(feat_made, 1)

            def aggregate(u, s, lo, hi):
                def window(of):
                    for j in range(TILES):
                        last = nc.tensor.matmul(ps_agg[0:D, 0:WINDOW], g[:, u, j * D:(j + 1) * D], of[:, j, :],
                                                start=(j == 0), stop=(j == TILES - 1))
                    return last
                with pe.If(hi >= lo + WINDOW):
                    with pe.Fori(lo + WINDOW, hi + 1, WINDOW) as w:
                        pe.wait_ge(far_onehot, rounds.next_far())
                        window(onehot_far).then_inc(far_made, 1)
                pe.wait_ge(onehot_ready, s + (RING + 1))
                pe.wait_ge(agg_added, s + RING)
                window(onehot).then_inc(agg_made, 1)

            def chunk_turn(layer, n):
                pe.wait_ge(ck_rows_in, n * 32 + 32)
                pe.wait_ge(ck_out_ready, n + 1)
                for k in range(KN):
                    last = nc.tensor.transpose(ps_ck[0:D, k * PN:(k + 1) * PN], ck_rows[:, k * D:(k + 1) * D],
                                               ident[0:PN, 0:PN])
                last.then_inc(ck_turned, 1)

            def chunk_first_product(layer, c, n):
                pe.wait_ge(ck_in_ready, n + 1)
                pe.wait_ge(ck_mid_ready, n + 1)
                to = ps_ck_mid[0:D, 0:CHUNK]
                if layer == 0:
                    nc.tensor.matmul(to, W1_s[:, :], ck_in[:, :], start=True, stop=True).then_inc(ck_mid_made, 1)
                else:
                    nc.tensor.matmul(to, Wn_s[:, :], aggB[:, chunk_cols(c)], start=True, stop=False)
                    nc.tensor.matmul(to, Ws_s[:, :], ck_in[:, :], start=False, stop=True).then_inc(ck_mid_made, 1)

            def chunk_last(layer, n):
                pe.wait_ge(ck_mid_ready, n + 2)
                if layer == 0:
                    nc.tensor.matmul(ps_ck[0:D, 0:CHUNK], W2_s[:, :], ck_mid[:, :], start=True, stop=True).then_inc(ck_out_made, 1)
                else:
                    for k in range(KN):
                        last = nc.tensor.transpose(ps_ck[0:PN, k * D:(k + 1) * D], ck_mid[:, k * PN:(k + 1) * PN],
                                                   ident[0:D, 0:D])
                    last.then_inc(ck_out_made, 1)

            def edges(layer, F, features, messages_ready):
                rounds.start_layer()
                turn_edges(0, layer * BLOCKS, layer * ROUNDS, F)
                features(0, 0, layer * BLOCKS)
                turn_edges(1, layer * BLOCKS + 1, layer * ROUNDS, F)

                def one_round(t):
                    rounds.load(t)
                    for u in range(RING):
                        final = isinstance(t, int)
                        s = t * RING + (u + layer * BLOCKS)
                        messages_ready(s)
                        aggregate(u, s, *rounds.reach(u))
                        if not (final and u == RING - 1):
                            features(t * RING + (u + 1), (u + 1) % RING, s + 1)
                        if not (final and u >= RING - 2):
                            turn_edges((u + 2) % RING, s + 2, t + (layer * ROUNDS + (u + 2) // RING), F)
                        if u < 3:
                            with pe.If(rounds.due() >= rounds.next_chunk() + 1):
                                c = rounds.due_chunk()
                                n = c + layer * CHUNKS
                                if u == 0:
                                    chunk_turn(layer, n)
                                if u == 1:
                                    chunk_first_product(layer, c, n)
                                if u == 2:
                                    chunk_last(layer, n)
                                    rounds.chunk_done()

                with pe.Fori(0, ROUNDS - 1) as t:
                    one_round(t)
                one_round(ROUNDS - 1)
                pe.wait_ge(agg_added, RING + (layer + 1) * BLOCKS)
                with pe.If(rounds.next_chunk() < CHUNKS):
                    with pe.Fori(rounds.next_chunk(), CHUNKS) as c:
                        n = c + layer * CHUNKS
                        chunk_turn(layer, n)
                        chunk_first_product(layer, c, n)
                        chunk_last(layer, n)

            edges(0, F0, features0, lambda s: pe.wait_ge(msg_ready, s + (RING + 1)))

            def turn_back(c, u):
                v = u % 2
                pe.wait_ge(z_ready, c + 1)
                chunk_reuse(pe, y_ready, c)
                for k in range(KN):
                    last = nc.tensor.transpose(ps_row[v][0:PN, k * D:(k + 1) * D], z[:, v, k * PN:(k + 1) * PN],
                                               ident[0:D, 0:D])
                last.then_inc(row_made, 1)
            each_chunk(pe, turn_back)

            edges(1, F1, features1, lambda s: pe.wait_ge(joined, s * 2 + (RING + 2)))

        @block.scalar
        def _(act):
            def permuted(t):
                return t.rearrange("d (k p) -> d k p", k=KN)

            def by_node(t):
                return t.rearrange("d (p k) -> d k p", k=KN)

            nc.scalar.memzero(aggA[:, :]).then_inc(tables_zeroed, 1)
            nc.scalar.memzero(aggB[:, :]).then_inc(tables_zeroed, 1)
            act.wait_ge(consts_set, 10)
            act.wait_ge(weights_in, 16 * WEIGHT_DMAS)
            act.wait_ge(meta_set, 3)
            rounds = Rounds(act, "act", 1)

            def edge_features(u, s, rows, read_by, read_count):
                act.wait_ge(eaT_made, s + (RING + 1))
                act.wait_ge(read_by, read_count)
                nc.scalar.copy(eaT[0:rows, u % 2, :], ps_eaT[0:rows, 0:2 * P]).then_inc(eaT_ready, 1)

            def hidden0(n):
                act.wait_ge(ck_mid_made, n + 2)
                act.wait_ge(ck_out_made, n + 1)
                nc.scalar.activation(ck_mid[:, :], ps_ck_mid[0:D, 0:CHUNK], ACT.Relu, bias=b1_c).then_inc(ck_mid_ready, 1)

            def input1(n):
                act.wait_ge(ck_turned, n + 1)
                act.wait_ge(ck_mid_made, n + 1)
                nc.scalar.copy(by_node(ck_in[:, :]), permuted(ps_ck[0:D, 0:CHUNK])).then_inc(ck_in_ready, 1)

            def hidden1(n):
                act.wait_ge(ck_mid_made, n + 2)
                act.wait_ge(ck_out_made, n + 1)
                nc.scalar.activation(permuted(ck_mid[:, :]), by_node(ps_ck_mid[0:D, 0:CHUNK]), ACT.Relu,
                                     bias=bias_out[:, :]).then_inc(ck_mid_ready, 1)

            def deviations1(c):
                act.wait_ge(ck_lnmv_ready, c + 1)
                nc.scalar.activation(ck_lnsd[:, :], ck_lnmv[:, :, 1], ACT.Sqrt, bias=eps_c[0:PN, :]).then_inc(ck_lnsd_ready, 1)

            def edges(layer, one_block, stages):
                rounds.start_layer()
                with act.Fori(0, ROUNDS) as t:
                    rounds.load(t, META_DUE)
                    for u in range(RING):
                        one_block(t * RING + u, u, t * RING + (u + layer * BLOCKS))
                        if u in stages:
                            with act.If(rounds.due() >= rounds.next_chunk() + 1):
                                c = rounds.due_chunk()
                                stages[u](c, c + layer * CHUNKS)
                                if u == max(stages):
                                    rounds.chunk_done()
                with act.If(rounds.next_chunk() < CHUNKS):
                    with act.Fori(rounds.next_chunk(), CHUNKS) as c:
                        for u in sorted(stages):
                            stages[u](c, c + layer * CHUNKS)

            def block0(b, u, s):
                edge_features(u, s, HALF * F0, feat_made, s * 2 + (RING - 2))
                act.wait_ge(joined, s * 2 + (RING + 2))
                nc.scalar.activation(g[:, u, :], g[:, u, :], ACT.Relu).then_inc(msg_ready, 1)

            def block1(b, u, s):
                edge_features(u, s, HALF * F1, h_made, b * 2 + (RING - 2))
                for h in range(2):
                    act.wait_ge(h_made, b * 2 + (RING + h + 1))
                    act.wait_ge(feat_made, s * 2 + (RING + h - 1))
                    nc.scalar.activation(hT[0:D, h * HALF * P:(h + 1) * HALF * P], ps_h[h][0:D, :], ACT.Relu,
                                         bias=c1_c).then_inc(hT_ready, 1)

            edges(0, block0, {2: lambda c, n: hidden0(n)})

            def normalize_roots(c, v):
                act.wait_ge(lnmv_ready, c + 1)
                nc.scalar.activation(lnsd[:, v, :], lnmv[:, v, :, 1], ACT.Sqrt, bias=eps_c[0:PN, :]).then_inc(lnsd_ready, 1)

            act.wait_ge(bn_step, 1)
            nc.scalar.activation(bn_tmp[:, 0:1], bnmv[:, 1:2], ACT.Sqrt, bias=eps_c[0:D, :]).then_inc(bn_step, 1)
            act.wait_ge(bn_step, 6)

            def batch_norm(c, u):
                v = u % 2
                chunk_reuse(act, row_made, c)
                nc.scalar.activation(permuted(z[:, v, :]), by_node(aggA[:, chunk_cols(c)]),
                                     ACT.Relu, bias=shift_bn[:, :], scale=scale_bn[:, :]).then_inc(z_ready, 1)
                if not (isinstance(c, int) and c == 0):
                    normalize_roots(c - 1, 1 - v)
            each_chunk(act, batch_norm)
            normalize_roots(CHUNKS - 1, 0)

            edges(1, block1, {1: lambda c, n: input1(n), 2: lambda c, n: hidden1(n), 3: lambda c, n: deviations1(c)})

        @block.vector
        def _(dve):
            src_v = src_all[:, :].rearrange("p (b j) -> p b j", j=TILES)
            rel_v = rel_all[:, :].rearrange("p (b j) -> p b j", j=TILES)
            for n in range(4):
                nb = BLK_B if n % 2 else BLK_A
                dve.wait_ge(idx_rows_in[n], 48 if n % 2 else 16)
                nc.vector.tensor_copy(rowsf[0:nb, n, :], raw[n]).then_inc(rows_cast, 1)
                if n == 1:
                    for q in range(4):
                        m, j0 = IDX_GROUPS[q]
                        b0, nb = (BLK_A, BLK_B) if m % 2 else (0, BLK_A)
                        dve.wait_ge(idx_turned, q + 1)
                        nc.vector.tensor_copy(src_v[:, b0:b0 + nb, j0:j0 + HALF],
                                              bank[2 + q % 6][:, :].rearrange("p (j b) -> p b j", j=HALF)[:, 0:nb, :]
                                              ).then_inc(idx_taken, 1)
                        if q == 1:
                            dve.wait_ge(idx_taken, 2)
                            for u in range(RING):
                                nc.vector.tensor_copy(idx[:, u, :], src_v[:, u, :]).then_inc(idx_ready, 1)
                    nc.vector.tensor_copy(src_v[:, BLOCKS:BLOCKS + RING, :], src_v[:, 0:RING, :]).then_inc(idx_taken, 1)
            for a, nb in ((0, BLK_A), (1, BLK_B)):
                dve.wait_ge(rows_cast, 3 + a)
                for t, op in ((0, ALU.min), (1, ALU.max)):
                    nc.vector.tensor_reduce(reach[0:nb, a, t:t + 1], rowsf[0:nb, 2 + a, :], axis=AX.X, op=op).then_inc(reach_set, 1)
            dve.wait_ge(reach_set, 4)
            dve.wait_ge(consts_set, 2)
            for t in range(2):
                for a, nb in ((0, BLK_A), (1, BLK_B)):
                    nc.vector.tensor_scalar(diag[0:nb, 2 * t + a, 0:nb], ident[0:nb, 0:nb], reach[0:nb, a, t:t + 1], None,
                                            ALU.mult).then_inc(diag_set, 1)
            dve.wait_ge(idx_turned, len(IDX_GROUPS) + 1)
            nc.vector.tensor_copy(lo_all[:, :], bank[4][:, 0:BLOCKS]).then_inc(diag_set, 1)
            meta_v = meta[:, :].rearrange("o (t m) -> o t m", m=META)
            for t in range(2):
                nc.vector.tensor_copy(meta_v[:, :, t * RING:(t + 1) * RING],
                                      bank[4][0:1, t * 2 * P:t * 2 * P + BLOCKS].rearrange("o (t u) -> o t u", u=RING)
                                      ).then_inc(meta_set, 1)
            dve.wait_ge(diag_set, 5)
            nc.vector.tensor_reduce(least[:, 0, :], lo_all[0:CHUNKS, :].rearrange("p (t u) -> p t u", u=RING), axis=AX.X,
                                    op=ALU.min).then_inc(least_set, 1)
            for q in range(4, 8):
                m, j0 = IDX_GROUPS[q]
                b0, nb = (BLK_A, BLK_B) if m % 2 else (0, BLK_A)
                for k in range(HALF):
                    last = nc.vector.tensor_tensor(rel_v[:, b0:b0 + nb, j0 + k], bank[2 + q % 6][:, k * P:k * P + nb],
                                                   lo_all[:, b0:b0 + nb], ALU.subtract)
                last.then_inc(idx_taken, 1)
            for n, shift in enumerate(SHIFTS):
                a, b = least[:, n % 2, :], least[:, (n + 1) % 2, :]
                dve.wait_ge(least_set, 2 * n + 1)
                nc.vector.tensor_copy(b[:, ROUNDS - shift:], a[:, ROUNDS - shift:]).then_inc(least_set, 1)
                nc.vector.tensor_tensor(b[:, 0:ROUNDS - shift], a[:, 0:ROUNDS - shift], a[:, shift:], ALU.min).then_inc(least_set, 1)
            dve.wait_ge(least_set, 2 * len(SHIFTS) + 1)
            dve.wait_ge(consts_set, 10)
            nc.vector.tensor_scalar(passed[:, :], least[:, len(SHIFTS) % 2, :], chunk_end[:, :], None,
                                    ALU.is_ge).then_inc(least_set, 1)
            dve.wait_ge(idx_turned, len(IDX_GROUPS) + 2)
            nc.vector.tensor_copy(meta_v[:, :, META_DUE], bank[1][0:1, 0:ROUNDS]).then_inc(meta_set, 1)
            dve.wait_ge(idx_taken, 9)
            nc.vector.memset(rel_v[0:SHARED, BLOCKS - 1, :], -1.0).then_inc(tables_zeroed, 1)
            dve.wait_ge(weights_in, 16 * WEIGHT_DMAS)
            nc.vector.tensor_tensor(bias_out[:, :], bs_c, bn_c, ALU.add).then_inc(bias_set, 1)
            for k in range(3):
                nc.vector.tensor_copy(be_part[:, k, :], be_left[:, k, :]).then_inc(be_split, 1)
                dve.wait_ge(be_split, 2 * k + 1)
                if k < 2:
                    nc.vector.tensor_tensor(be_left[:, k + 1, :], be_left[:, k, :], be_part[:, k, :], ALU.subtract).then_inc(be_split, 1)
                    dve.wait_ge(be_split, 2 * k + 2)
            nc.vector.tensor_scalar(be_left[:, 0, :], be_part[:, 0, :], ident[0:3, 0:1], None, ALU.mult).then_inc(be_split, 1)
            for k in (1, 2):
                dve.wait_ge(be_split, 5 + k)
                nc.vector.scalar_tensor_tensor(out=be_left[:, k, :], in0=be_part[:, k, :], scalar=ident[0:3, k:k + 1],
                                               in1=be_left[:, k - 1, :], op0=ALU.mult, op1=ALU.add).then_inc(be_split, 1)
            dve.wait_ge(be_split, 8)
            nc.vector.tensor_copy(be_rows[0:3, :], be_left[:, 2, :]).then_inc(be_split, 1)
            dve.wait_ge(tables_zeroed, 3)
            dve.wait_ge(meta_set, 3)
            rounds = Rounds(dve, "dve", META_DUE + 1)

            def input0(c, n):
                dve.wait_ge(ck_turned, n + 1)
                dve.wait_ge(ck_mid_made, n + 1)
                nc.vector.tensor_tensor(ck_in[:, :].rearrange("d (p k) -> d k p", k=KN),
                                        ps_ck[0:D, 0:CHUNK].rearrange("d (k p) -> d k p", k=KN),
                                        aggA[:, chunk_cols(c)].rearrange("d (p k) -> d k p", k=KN),
                                        ALU.add).then_inc(ck_in_ready, 1)

            def result0(c, n):
                chunk = aggA[:, chunk_cols(c)]
                dve.wait_ge(ck_out_made, n + 2)
                nc.vector.tensor_scalar(chunk, ps_ck[0:D, 0:CHUNK], b2_c, None, ALU.add).then_inc(ck_out_ready, 1)
                dve.wait_ge(ck_out_ready, n + 2)
                nc.vector.bn_stats(bnst[:, ds(c * 6, 6)], chunk).then_inc(stats_ready, 1)

            def result1(c, n):
                dve.wait_ge(ck_out_made, n + 2)
                nc.vector.tensor_tensor(ck_y[:, :], ps_ck[0:PN, 0:KN * D], ck_rows[:, :], ALU.add).then_inc(ck_out_ready, 1)
                dve.wait_ge(ck_out_ready, n + 2)
                for k in range(KN):
                    last = nc.vector.bn_stats(ck_lnst[:, 6 * k:6 * k + 6], ck_y[:, k * D:(k + 1) * D])
                last.then_inc(ck_lnst_ready, 1)
                dve.wait_ge(ck_lnst_ready, c + 1)
                dve.sem_inc(dve_waited, 1)
                for k in range(KN):
                    last = nc.vector.bn_aggr(ck_lnmv[:, k, :], ck_lnst[:, 6 * k:6 * k + 6])
                last.then_inc(ck_lnmv_ready, 1)

            def normalized1(c, n):
                dve.wait_ge(ck_lnsd_ready, c + 1)
                nc.vector.reciprocal(ck_lnrs[:, :], ck_lnsd[:, :]).then_inc(ck_lnrs_ready, 1)
                dve.wait_ge(ck_lnrs_ready, c + 1)
                nc.vector.scalar_tensor_tensor(out=ck_lnnb[:, :], in0=ck_lnmv[:, :, 0], scalar=-1.0, in1=ck_lnrs[:, :],
                                               op0=ALU.mult, op1=ALU.mult).then_inc(ck_lnnb_ready, 1)
                dve.wait_ge(ck_lnnb_ready, c + 1)
                dve.wait_ge(ck_yn_free, c + 1)
                for k in range(KN):
                    last = nc.vector.tensor_scalar(ck_yn[:, k * D:(k + 1) * D], ck_y[:, k * D:(k + 1) * D],
                                                   ck_lnrs[:, k:k + 1], ck_lnnb[:, k:k + 1], ALU.mult, ALU.add)
                last.then_inc(ck_yn_ready, 1)

            def edges(layer, op, early, late):
                agg = (aggA, aggB)[layer]
                rounds.start_layer()

                def build_onehot(to, of):
                    for j in range(TILES):
                        last = nc.vector.tensor_scalar(to[:, j, :], iota_row[:, :], of[:, j:j + 1], None, ALU.is_equal)
                    return last

                def add_window(start):
                    return nc.vector.tensor_tensor(agg[:, ds(start, WINDOW)], ps_agg[0:D, 0:WINDOW],
                                                   agg[:, ds(start, WINDOW)], ALU.add)

                with dve.Fori(0, ROUNDS) as t:
                    rounds.load(t)
                    for u in range(RING):
                        b = t * RING + u
                        s = t * RING + (u + layer * BLOCKS)
                        lo, hi = rounds.reach(u)
                        nc.vector.tensor_copy(rel[:, :], rel_all[:, ds(b * TILES, TILES)]).then_inc(rel_set, 1)
                        nc.vector.tensor_copy(rel_far[:, :], rel_all[:, ds(b * TILES, TILES)]).then_inc(rel_set, 1)
                        dve.wait_ge(rel_set, s * 2 + (RING + 2))
                        build_onehot(onehot, rel).then_inc(onehot_ready, 1)
                        if u in early:
                            with dve.If(rounds.due() >= rounds.next_chunk() + 1):
                                c = rounds.due_chunk()
                                early[u](c, c + layer * CHUNKS)
                        dve.wait_ge(rows_in[u], t * (16 * TILES) + (layer * ROUNDS + 1) * (16 * TILES))
                        for h in range(2):
                            half = g[:, u, h * HALF * D:(h + 1) * HALF * D]
                            dve.wait_ge(feat_made, s * 2 + (RING + h + 1))
                            nc.vector.tensor_tensor(half, ps_feat[h][:, 0:HALF * D], half, op).then_inc(joined, 1)
                        nc.vector.tensor_copy(idx[:, u, :], src_all[:, ds((b + RING) * TILES, TILES)]).then_inc(idx_ready, 1)
                        with dve.If(hi >= lo + WINDOW):
                            with dve.Fori(lo + WINDOW, hi + 1, WINDOW) as w:
                                f = rounds.next_far()
                                nc.vector.tensor_scalar(rel_far[:, :], rel_far[:, :], -float(WINDOW), None,
                                                        ALU.add).then_inc(far_rel_set, 1)
                                dve.wait_ge(far_rel_set, f)
                                build_onehot(onehot_far, rel_far).then_inc(far_onehot, 1)
                                dve.wait_ge(far_made, f)
                                add_window(w).then_inc(far_added, 1)
                                dve.wait_ge(far_added, f)
                        dve.wait_ge(agg_made, s + (RING + 1))
                        add_window(lo).then_inc(agg_added, 1)
                        dve.wait_ge(agg_added, s + (RING + 1))
                        if u in late or u == RING - 1:
                            with dve.If(rounds.due() >= rounds.next_chunk() + 1):
                                if u in late:
                                    c = rounds.due_chunk()
                                    late[u](c, c + layer * CHUNKS)
                                if u == RING - 1:
                                    rounds.chunk_done()
                with dve.If(rounds.next_chunk() < CHUNKS):
                    with dve.Fori(rounds.next_chunk(), CHUNKS) as c:
                        for stage in (*early.values(), *late.values()):
                            stage(c, c + layer * CHUNKS)

            edges(0, ALU.add, {1: input0, 3: result0}, {})

            dve.wait_ge(stats_ready, CHUNKS)
            nc.vector.bn_aggr(bnmv[:, :], bnst[:, :]).then_inc(bn_step, 1)
            dve.wait_ge(bn_step, 2)
            nc.vector.reciprocal(bn_tmp[:, 1:2], bn_tmp[:, 0:1]).then_inc(bn_step, 1)
            dve.wait_ge(bn_step, 3)
            nc.vector.tensor_tensor(scale_bn[:, :], bn_tmp[:, 1:2], gamma_c, ALU.mult).then_inc(bn_step, 1)
            dve.wait_ge(bn_step, 4)
            nc.vector.scalar_tensor_tensor(out=shift_bn[:, :], in0=bnmv[:, 0:1], scalar=-1.0, in1=scale_bn[:, :],
                                           op0=ALU.mult, op1=ALU.mult).then_inc(bn_step, 1)
            dve.wait_ge(bn_step, 5)
            nc.vector.tensor_tensor(shift_bn[:, :], shift_bn[:, :], beta_c, ALU.add).then_inc(bn_step, 1)

            def stats(c, u):
                v = u % 2
                dve.wait_ge(row_made, c + 1)
                dve.wait_ge(xr_in[u], 32 * (c // RING + 1) if isinstance(c, int) else (c - u) * (32 // RING) + 32)
                chunk_reuse(dve, yn_ready, c)
                nc.vector.tensor_tensor(y[:, v, :], ps_row[v][0:PN, 0:KN * D], xr[:, u, :], ALU.add).then_inc(y_ready, 1)
                dve.wait_ge(y_ready, c + 1)
                for k in range(KN):
                    last = nc.vector.bn_stats(lnst[:, v, 6 * k:6 * k + 6], y[:, v, k * D:(k + 1) * D])
                last.then_inc(lnst_ready, 1)
                dve.wait_ge(lnst_ready, c + 1)
                chunk_reuse(dve, lnsd_ready, c)
                dve.sem_inc(dve_waited, 1)
                for k in range(KN):
                    last = nc.vector.bn_aggr(lnmv[:, v, k, :], lnst[:, v, 6 * k:6 * k + 6])
                last.then_inc(lnmv_ready, 1)

            def factors(c, v):
                dve.wait_ge(lnsd_ready, c + 1)
                nc.vector.reciprocal(lnrs[:, v, :], lnsd[:, v, :]).then_inc(lnrs_ready, 1)
                dve.wait_ge(lnrs_ready, c + 1)
                nc.vector.scalar_tensor_tensor(out=lnnb[:, v, :], in0=lnmv[:, v, :, 0], scalar=-1.0, in1=lnrs[:, v, :],
                                               op0=ALU.mult, op1=ALU.mult).then_inc(lnnb_ready, 1)

            def norm_chunk(c, u):
                stats(c, u)
                if not (isinstance(c, int) and c == 0):
                    factors(c - 1, 1 - u % 2)
            each_chunk(dve, norm_chunk)
            factors(CHUNKS - 1, 0)

            edges(1, ALU.mult, {3: result1}, {3: normalized1})


_INS = ['x', 'src', 'dst', 'edge_attr_17', 'edge_attr_32', 'L0_gnn_We', 'L0_gnn_be', 'L0_gnn_W1', 'L0_gnn_b1',
        'L0_gnn_W2', 'L0_gnn_b2', 'L0_gnn_gamma', 'L0_gnn_beta', 'L1_gnn_W1', 'L1_gnn_b1', 'L1_gnn_W2', 'L1_gnn_b2',
        'L1_gnn_Ws', 'L1_gnn_bs', 'L1_gnn_Wn', 'L1_gnn_bn']
_TRANSPOSED = ('L1_gnn_W1', 'L1_gnn_W2', 'L1_gnn_Ws', 'L1_gnn_Wn')
_OUTS = [((12500, 96), 'float32')]


def kernel(**inputs):
    import numpy as _np
    import concourse.bacc as _bacc
    from concourse import mybir as _mybir
    from concourse.bass_utils import run_bass_kernel_spmd as _run

    nc = _bacc.Bacc("TRN2", target_bir_lowering=False, num_devices=1)
    arrays, args = {}, []
    for name in _INS:
        a = _np.asarray(inputs[name])
        a = _np.ascontiguousarray(a.T if name in _TRANSPOSED else a)
        arrays[f"in_{name}_dram"] = a
        args.append(nc.dram_tensor(f"in_{name}_dram", a.shape, _mybir.dt.from_np(a.dtype), kind="ExternalInput").ap())
    for i, (shape, dtype) in enumerate(_OUTS):
        dt = _mybir.dt.from_np(_np.dtype(dtype))
        args.append(nc.dram_tensor(f"out_{i}_dram", shape, dt, kind="ExternalOutput").ap())
    gnn_two_layers_kernel(nc, *args)
    r = _run(nc, [arrays], core_ids=[0])
    got = tuple(r.results[0][f"out_{i}_dram"] for i in range(len(_OUTS)))
    return got[0]
```

```python
import concourse.bass as bass
from concourse import mybir
from contextlib import ExitStack


def gnn_two_layers_kernel(
    nc: bass.Bass,
    x: bass.AP,
    src: bass.AP,
    dst: bass.AP,
    edge_attr_17: bass.AP,
    edge_attr_32: bass.AP,
    We: bass.AP,
    be: bass.AP,
    W1: bass.AP,
    b1: bass.AP,
    W2: bass.AP,
    b2: bass.AP,
    gamma: bass.AP,
    beta: bass.AP,
    V1T: bass.AP,
    c1: bass.AP,
    V2T: bass.AP,
    c2: bass.AP,
    WsT: bass.AP,
    bs: bass.AP,
    WnT: bass.AP,
    bn: bass.AP,
    out: bass.AP,
):
    f32 = mybir.dt.float32
    bf16 = mybir.dt.bfloat16
    i32 = mybir.dt.int32
    u32 = mybir.dt.uint32
    ALU = mybir.AluOpType
    ACT = mybir.ActivationFunctionType
    AX = mybir.AxisListType
    ds = bass.ds

    P = 128
    N, D = x.shape
    E, F0 = edge_attr_32.shape
    F1 = edge_attr_17.shape[1]
    TILES = 8
    HALF = TILES // 2
    BLOCK = P * TILES
    BLOCKS = -(-E // BLOCK)
    RING = 4
    ROUNDS = BLOCKS // RING
    assert ROUNDS * RING == BLOCKS
    WINDOW = 96
    META = 12
    SHARED = (BLOCKS * BLOCK - E) // TILES
    EPS = 1e-5

    KN = 4
    POOL_KN = 3
    PN = 125
    CHUNK = KN * PN
    CHUNKS = N // CHUNK
    CHUNK_ROUNDS = CHUNKS // RING
    assert CHUNKS * CHUNK == N and CHUNKS == CHUNK_ROUNDS * RING + 1
    SPLIT = 112
    BLK_A = P
    BLK_B = BLOCKS - BLK_A

    ea_rows = [edge_attr_32.rearrange("(r j) f -> r (j f)", j=TILES),
               edge_attr_17.rearrange("(r j) f -> r (j f)", j=TILES)]
    EA_LAST = E // TILES - P
    x1 = nc.dram_tensor("x1_rows", (N, D), f32).ap()

    ctx = ExitStack()
    with ctx:
        def sb(name, shape, dt=f32):
            return ctx.enter_context(nc.sbuf_tensor(name, shape, dt))

        def sem(name):
            return ctx.enter_context(nc.semaphore(name))

        ident = sb("ident", [P, P])
        ones = sb("ones", [P, P])
        iota_row = sb("iota_row", [P, WINDOW])
        We_diag = sb("We_diag", [P, HALF * D])
        be_rows = sb("be_rows", [P, HALF * D], bf16)
        pick3 = sb("pick3", [P, P], bf16)
        be_left = sb("be_left", [3, 3, HALF * D])
        be_part = sb("be_part", [3, 3, HALF * D], bf16)
        W1_s = sb("W1_s", [D, D])
        W2_s = sb("W2_s", [D, D])
        V1_pad = sb("V1_pad", [HALF * F1, HALF, D])
        V2_s = sb("V2_s", [D + 1, D])
        Ws_s = sb("Ws_s", [D, D])
        Wn_s = sb("Wn_s", [D, D])
        cols = sb("cols", [D, 8])
        b1_c, b2_c, gamma_c, beta_c, c1_c, bs_c, bn_c = (cols[:, n:n + 1] for n in range(7))
        eps_c = sb("eps_c", [P, 1])
        bias_out = sb("bias_out", [D, 1])
        scale_bn = sb("scale_bn", [D, 1])
        shift_bn = sb("shift_bn", [D, 1])
        bn_tmp = sb("bn_tmp", [D, 2])

        shared = sb("shared", [P, 4 * BLOCK])
        raw = [shared[0:nb, n * BLOCK:(n + 1) * BLOCK].bitcast(i32)
               for n, nb in enumerate((BLK_A, BLK_B, BLK_A, BLK_B))]
        z = shared[0:D, 0:2 * CHUNK].rearrange("d (v n) -> d v n", v=2)
        xr = shared[0:PN, 2 * CHUNK:2 * CHUNK + RING * KN * D].rearrange("p (v n) -> p v n", v=RING)

        shared_f = sb("shared_f", [P, 4 * BLOCK])
        rowsf = shared_f[:, :].rearrange("p (n b) -> p n b", n=4)
        y, yn = (shared_f[0:PN, n * RING * KN * D:(n + 1) * RING * KN * D].rearrange("p (v n) -> p v n", v=RING)
                 for n in range(2))
        reach = sb("reach", [P, 2, 2])
        meta = sb("meta", [1, ROUNDS * META], i32)
        diag = sb("diag", [P, 4, P])
        lo_all = sb("lo_all", [P, BLOCKS])
        least = sb("least", [CHUNKS, 2, ROUNDS])
        chunk_end = sb("chunk_end", [CHUNKS, 1])
        passed = sb("passed", [CHUNKS, ROUNDS])
        src_all = sb("src_all", [P, (BLOCKS + RING) * TILES], i32)
        rel_all = sb("rel_all", [P, BLOCKS * TILES])

        aggA = sb("aggA", [D, N + WINDOW])
        aggB = sb("aggB", [D, N + WINDOW])

        idx = sb("idx", [P, RING, TILES], i32)
        g = sb("g", [P, RING, TILES * D])
        ea = sb("ea", [P, RING, TILES * F0])
        eaT = sb("eaT", [P, 2, 2 * P])
        hT = sb("hT", [D + 1, BLOCK])
        rel = sb("rel", [P, TILES])
        rel_far = sb("rel_far", [P, TILES])
        onehot = sb("onehot", [P, TILES, WINDOW])
        onehot_far = sb("onehot_far", [P, TILES, WINDOW])

        ck_rows = sb("ck_rows", [PN, KN * D])
        ck_in = sb("ck_in", [D, CHUNK])
        ck_mid = sb("ck_mid", [D, CHUNK])
        ck_y = sb("ck_y", [PN, KN * D])
        ck_yn = sb("ck_yn", [PN, KN * D])
        ck_lnst = sb("ck_lnst", [PN, KN * 6])
        ck_lnmv = sb("ck_lnmv", [PN, KN, 2])
        ck_lnsd = sb("ck_lnsd", [PN, KN])
        ck_lnrs = sb("ck_lnrs", [PN, KN])
        ck_lnnb = sb("ck_lnnb", [PN, KN])

        bnst = sb("bnst", [D, CHUNKS * 6])
        bnmv = sb("bnmv", [D, 2])
        lnst = sb("lnst", [PN, RING, KN * 6])
        lnmv = sb("lnmv", [PN, RING, KN, 2])
        lnsd = sb("lnsd", [PN, RING, KN])
        lnrs = sb("lnrs", [PN, RING, KN])
        lnnb = sb("lnnb", [PN, RING, KN])

        bank = [ctx.enter_context(nc.psum_tensor(f"bank{n}", [P, 512], f32)) for n in range(8)]
        ps_eaT = bank[0]
        ps_ck = bank[1]
        ps_ck_mid = bank[7]
        ps_feat = bank[2:4]
        ps_h = bank[4:6]
        ps_agg = bank[6]
        ps_row = bank[4:6]

        first_idx_in = sem("first_idx_in")
        idx_rows_in = [sem(f"idx_rows_in{n}") for n in range(4)]
        weights_in = sem("weights_in")
        meta_set = sem("meta_set")
        least_set = sem("least_set")
        be_split = sem("be_split")
        consts_set = sem("consts_set")
        pads_set = sem("pads_set")
        tables_zeroed = sem("tables_zeroed")
        rows_cast = sem("rows_cast")
        reach_set = sem("reach_set")
        diag_set = sem("diag_set")
        idx_turned = sem("idx_turned")
        idx_taken = sem("idx_taken")
        bias_set = sem("bias_set")
        pool_waited = sem("pool_waited")
        dve_waited = sem("dve_waited")
        ea_in = [sem(f"ea_in{n}") for n in range(RING)]
        rows_in = [[sem(f"rows_in{n}_{h}") for h in range(2)] for n in range(RING)]
        idx_ready = sem("idx_ready")
        eaT_made = sem("eaT_made")
        eaT_ready = sem("eaT_ready")
        h_made = sem("h_made")
        hT_ready = sem("hT_ready")
        feat_made = sem("feat_made")
        joined = sem("joined")
        msg_ready = sem("msg_ready")
        rel_set = sem("rel_set")
        onehot_ready = sem("onehot_ready")
        agg_made = sem("agg_made")
        agg_added = sem("agg_added")
        far_rel_set = sem("far_rel_set")
        far_onehot = sem("far_onehot")
        far_made = sem("far_made")
        far_added = sem("far_added")
        ck_rows_in = sem("ck_rows_in")
        ck_turned = sem("ck_turned")
        ck_in_ready = sem("ck_in_ready")
        ck_mid_made = sem("ck_mid_made")
        ck_mid_ready = sem("ck_mid_ready")
        ck_out_made = sem("ck_out_made")
        ck_out_ready = sem("ck_out_ready")
        ck_lnst_ready = sem("ck_lnst_ready")
        ck_lnmv_ready = sem("ck_lnmv_ready")
        ck_lnsd_ready = sem("ck_lnsd_ready")
        ck_lnrs_ready = sem("ck_lnrs_ready")
        ck_lnnb_ready = sem("ck_lnnb_ready")
        ck_yn_ready = sem("ck_yn_ready")
        ck_yn_free = sem("ck_yn_free")
        ck_stored = sem("ck_stored")
        xr_in = [sem(f"xr_in{n}") for n in range(RING)]
        stats_ready = sem("stats_ready")
        bn_step = sem("bn_step")
        z_ready = sem("z_ready")
        row_made = sem("row_made")
        y_ready = sem("y_ready")
        lnst_ready = sem("lnst_ready")
        lnmv_ready = sem("lnmv_ready")
        lnsd_ready = sem("lnsd_ready")
        lnrs_ready = sem("lnrs_ready")
        lnnb_ready = sem("lnnb_ready")
        yn_ready = sem("yn_ready")
        yn_ready_act = sem("yn_ready_act")
        stored = [sem(f"stored{n}") for n in range(RING)]

        WEIGHT_DMAS = 3 * HALF + 4 + 2 + 7
        STORES = [32 * len(range(n, CHUNKS, RING)) for n in range(RING)]
        IDX_GROUPS = [(n, j0) for n in range(4) for j0 in (0, HALF)]
        SHIFTS = [1 << n for n in range((ROUNDS - 1).bit_length())]
        PASSED_SET = 2 * len(SHIFTS) + 2
        META_DUE = 2 * RING

        def each_chunk(eng, body):
            for u in range(RING):
                body(u, u)
            with eng.Fori(1, CHUNK_ROUNDS) as t:
                for u in range(RING):
                    body(t * RING + u, u)
            body(CHUNKS - 1, 0)

        def chunk_reuse(eng, semaphore, c, slots=2):
            if not (isinstance(c, int) and c < slots):
                eng.wait_ge(semaphore, c - (slots - 1))

        def lag(c, steps):
            return not (isinstance(c, int) and c < steps)

        def uses_before(c, u):
            return 32 * (c // RING) if isinstance(c, int) else (c - u) * (32 // RING)

        class Rounds:

            def __init__(self, eng, name, values):
                self.eng = eng
                self.table = [eng.alloc_register(f"{name}_table{n}") for n in range(values)]
                self.chunk = eng.alloc_register(f"{name}_chunk")
                self.far = eng.alloc_register(f"{name}_far")
                eng.reg_mov(self.far, 0)

            def start_layer(self):
                self.eng.reg_mov(self.chunk, 0)

            def load(self, t, at=0):
                self.eng.load(self.table, meta[0:1, ds(t * META + at, len(self.table))])

            def reach(self, u):
                return (self.eng.snap(self.table[u], min_val=0, max_val=N - 1),
                        self.eng.snap(self.table[RING + u], min_val=0, max_val=N - 1))

            def due(self):
                return self.eng.snap(self.table[-1], min_val=0, max_val=CHUNKS)

            def next_chunk(self):
                return self.eng.snap(self.chunk, min_val=0, max_val=CHUNKS)

            def due_chunk(self):
                return self.eng.snap(self.chunk, min_val=0, max_val=CHUNKS - 1)

            def chunk_done(self):
                self.eng.reg_add(self.chunk, self.chunk, 1)

            def next_far(self):
                self.eng.reg_add(self.far, self.far, 1)
                return self.eng.snap(self.far, min_val=1)

        def chunk_cols(c):
            return ds(c * CHUNK, CHUNK)

        block = ctx.enter_context(nc.Block())

        @block.sync
        def _(sp):
            def rows_of(table):
                return table.rearrange("(q k) f -> q (k f)", k=KN)

            def load_chunk(tile, table, c, semaphore):
                rows = rows_of(table)
                sp.dma_start(tile[0:SPLIT, :], rows[ds(c * PN, SPLIT), :]).then_inc(semaphore, 16)
                sp.dma_start(tile[SPLIT:PN, :], rows[ds(c * PN + SPLIT, PN - SPLIT), :]).then_inc(semaphore, 16)

            def store_chunk(table, c, tile, semaphore):
                rows = rows_of(table)
                sp.dma_start(rows[ds(c * PN, SPLIT), :], tile[0:SPLIT, :]).then_inc(semaphore, 16)
                sp.dma_start(rows[ds(c * PN + SPLIT, PN - SPLIT), :], tile[SPLIT:PN, :]).then_inc(semaphore, 16)

            sp.dma_start(idx[:, :, :], src[0:RING * BLOCK].rearrange("(u p j) -> p u j", p=P, j=TILES)).then_inc(first_idx_in, 16)
            full = (BLOCKS - 1 - BLK_A) // 16 * 16
            for n, (a, tA, tB) in enumerate([(src, raw[0], raw[1]), (dst, raw[2], raw[3])]):
                v = a[0:(BLOCKS - 1) * BLOCK].rearrange("(b e) -> b e", e=BLOCK)
                sp.dma_start(tA, v[0:BLK_A, :]).then_inc(idx_rows_in[2 * n], 16)
                sp.dma_start(tB[0:full, :], v[BLK_A:BLK_A + full, :]).then_inc(idx_rows_in[2 * n + 1], 16)
                sp.dma_start(tB[full:BLK_B - 1, :], v[BLK_A + full:BLOCKS - 1, :]).then_inc(idx_rows_in[2 * n + 1], 16)
                sp.dma_start(tB[BLK_B - 1:BLK_B, :],
                             a[E - BLOCK:E].rearrange("(b e) -> b e", e=BLOCK)).then_inc(idx_rows_in[2 * n + 1], 16)
            sp.wait_ge(pads_set, 2)
            for k in range(HALF):
                sp.dma_start(We_diag[k * F0:(k + 1) * F0, k * D:(k + 1) * D], We[:, :]).then_inc(weights_in, 16)
                sp.dma_start(be_left[:, 0, k * D:(k + 1) * D],
                             be.rearrange("(o d) -> o d", o=1).to_broadcast([3, D])).then_inc(weights_in, 16)
                sp.dma_start(V1_pad[k * F1:(k + 1) * F1, k, :], V1T[:, :]).then_inc(weights_in, 16)
            for tile, w in ((W1_s, W1), (W2_s, W2), (Ws_s, WsT), (Wn_s, WnT)):
                sp.dma_start(tile[:, :], w[:, :]).then_inc(weights_in, 16)
            sp.dma_start(V2_s[0:D, :], V2T[:, :]).then_inc(weights_in, 16)
            sp.dma_start(V2_s[D:D + 1, :], c2.rearrange("(o d) -> o d", o=1)).then_inc(weights_in, 16)
            for tile, w in ((b1_c, b1), (b2_c, b2), (gamma_c, gamma), (beta_c, beta), (c1_c, c1), (bs_c, bs), (bn_c, bn)):
                sp.dma_start(tile, w.rearrange("(d o) -> d o", o=1)).then_inc(weights_in, 16)

            rounds = Rounds(sp, "sp", 1)
            stores = sp.alloc_register("sp_stores")
            loaded = sp.alloc_register("sp_loaded")

            def edges(layer, F, table):
                rounds.start_layer()
                sp.reg_mov(stores, 0)

                def load_edges(start, u, s):
                    sp.wait_ge(eaT_made, s + 1)
                    sp.dma_start(ea[:, u, 0:TILES * F], ea_rows[layer][ds(start, P), :]).then_inc(ea_in[u], 16)

                def stored_so_far():
                    return sp.snap(stores, min_val=0, max_val=CHUNKS - 1)

                def store(c):
                    sp.wait_ge(ck_yn_ready, c + 1)
                    store_chunk(out, c, ck_yn, ck_stored)
                    sp.wait_ge(ck_stored, c * 32 + 32)
                    sp.sem_inc(ck_yn_free, 1)
                    sp.reg_add(stores, stores, 1)

                def load(c):
                    sp.wait_ge(ck_out_ready, c + (layer * CHUNKS + 1))
                    load_chunk(ck_rows, table, c, ck_rows_in)

                def one_round(t):
                    for u in range(RING):
                        last = isinstance(t, int) and t == ROUNDS - 1 and u == RING - 1
                        load_edges(EA_LAST if last else t * (RING * P) + u * P, u, t * RING + (u + layer * BLOCKS))
                    if layer == 0 and isinstance(t, int) and t == 0:
                        sp.wait_ge(meta_set, 3)
                    rounds.load(t, META_DUE)
                    sp.reg_mov(loaded, rounds.chunk)
                    with sp.If(rounds.due() >= rounds.next_chunk() + 1):
                        load(rounds.due_chunk())
                        rounds.chunk_done()
                    if layer:
                        store_if_behind()

                def store_if_behind():
                    with sp.If(sp.snap(loaded, min_val=0, max_val=CHUNKS) >= sp.snap(stores, min_val=0, max_val=CHUNKS) + 1):
                        store(stored_so_far())

                one_round(0)
                with sp.Fori(1, ROUNDS - 1) as t:
                    one_round(t)
                one_round(ROUNDS - 1)
                if layer:
                    sp.reg_mov(loaded, rounds.chunk)
                    store_if_behind()
                with sp.If(rounds.next_chunk() < CHUNKS):
                    with sp.Fori(rounds.next_chunk(), CHUNKS) as c:
                        load(c)
                        if layer:
                            store(c)

            edges(0, F0, x)

            def load(c, u):
                chunk_reuse(sp, y_ready, c, RING)
                sp.dma_start(xr[:, u, :], rows_of(x)[ds(c * PN, PN), :]).then_inc(xr_in[u], 16)

            def store(c, u):
                sp.wait_ge(yn_ready_act, c + (RING + 1))
                sp.wait_ge(yn_ready, c + (RING + 1))
                store_chunk(x1, c, yn[:, u, :], stored[u])

            AHEAD = 2 * RING - 1
            for c in range(AHEAD):
                load(c, c % RING)
            with sp.Fori(0, CHUNK_ROUNDS - 2) as t:
                for u in range(RING):
                    load(t * RING + (u + AHEAD), (u + AHEAD) % RING)
                    store(t * RING + u, u)
            for c in range((CHUNK_ROUNDS - 2) * RING, CHUNKS):
                if c + AHEAD < CHUNKS:
                    load(c + AHEAD, (c + AHEAD) % RING)
                store(c, c % RING)
            for n in range(RING):
                sp.wait_ge(stored[n], STORES[n])
            edges(1, F1, x1)
            sp.wait_ge(ck_stored, 32 * CHUNKS)

        @block.gpsimd
        def _(pool):
            nc.gpsimd.memset(ident[:, :], 0.0).then_inc(consts_set, 1)
            pool.wait_ge(consts_set, 1)
            nc.gpsimd.affine_select(out=ident[:, :], in_=ident[:, :], compare_op=ALU.not_equal, fill=1.0,
                                    base=0, pattern=[[-1, P]], channel_multiplier=1).then_inc(consts_set, 1)
            nc.gpsimd.memset(We_diag[:, :], 0.0).then_inc(pads_set, 1)
            nc.gpsimd.memset(V1_pad[:, :, :], 0.0).then_inc(pads_set, 1)
            nc.gpsimd.iota(iota_row[:, :], pattern=[[1, WINDOW]], base=0, channel_multiplier=0,
                           allow_small_or_imprecise_dtypes=True).then_inc(consts_set, 1)
            nc.gpsimd.memset(ones[:, :], 1.0).then_inc(consts_set, 1)
            nc.gpsimd.memset(pick3[:, :], 0.0).then_inc(consts_set, 1)
            nc.gpsimd.memset(be_rows[:, :], 0.0).then_inc(consts_set, 1)
            nc.gpsimd.iota(chunk_end[:, :], pattern=[[0, 1]], base=CHUNK, channel_multiplier=CHUNK,
                           allow_small_or_imprecise_dtypes=True).then_inc(consts_set, 1)
            pool.wait_ge(consts_set, 7)
            nc.gpsimd.memset(pick3[0:3, :], 1.0).then_inc(consts_set, 1)
            pool.wait_ge(consts_set, 8)
            nc.gpsimd.memset(hT[D:D + 1, :], 1.0).then_inc(consts_set, 1)
            pool.wait_ge(consts_set, 9)
            nc.gpsimd.memset(eps_c[:, :], EPS).then_inc(consts_set, 1)

            def gather(layer, table):
                with pool.Fori(0, ROUNDS) as t:
                    for u in range(RING):
                        s = t * RING + (u + layer * BLOCKS)
                        pool.wait_ge(idx_ready, s + 1)
                        pool.wait_ge(agg_made, s + 1)
                        pool.sem_inc(pool_waited, 1)
                        for j in range(TILES):
                            nc.gpsimd.indirect_dma_start(
                                out=g[:, u, j * D:(j + 1) * D], out_offset=None, in_=table[:, :],
                                in_offset=bass.IndirectOffsetOnAxis(ap=idx[:, u, j:j + 1].bitcast(u32), axis=0),
                            ).then_inc(rows_in[u][j // HALF], 16)

            def normalize(c, u):
                pool.wait_ge(lnnb_ready, c + 1)
                if lag(c, RING):
                    pool.wait_ge(stored[u], uses_before(c, u))
                pool.sem_inc(pool_waited, 1)
                for k in range(POOL_KN):
                    last = nc.gpsimd.tensor_scalar(yn[:, u, k * D:(k + 1) * D], y[:, u, k * D:(k + 1) * D],
                                                   lnrs[:, u, k:k + 1], lnnb[:, u, k:k + 1], ALU.mult, ALU.add)
                last.then_inc(yn_ready, 1)

            pool.wait_ge(first_idx_in, 16)
            pool.sem_inc(idx_ready, RING)
            gather(0, x)
            each_chunk(pool, normalize)
            for n in range(RING):
                pool.wait_ge(stored[n], STORES[n])
            gather(1, x1)

        @block.tensor
        def _(pe):
            for q in (eaT_made, eaT_ready, h_made, hT_ready, feat_made, joined, msg_ready, rel_set,
                      onehot_ready, agg_made, agg_added):
                pe.sem_inc(q, RING)
            for q in (ck_mid_made, ck_mid_ready, ck_out_made, ck_out_ready, ck_yn_free):
                pe.sem_inc(q, 1)
            for q, lead in ((lnst_ready, 1), (lnsd_ready, 2), (lnrs_ready, 2), (yn_ready, RING), (yn_ready_act, RING)):
                pe.sem_inc(q, lead)

            pe.wait_ge(consts_set, 2)
            for q, (n, j0) in enumerate(IDX_GROUPS):
                nb = BLK_B if n % 2 else BLK_A
                pe.wait_ge(rows_cast, n + 1)
                if q >= 6:
                    pe.wait_ge(idx_taken, q - 5)
                for k in range(HALF):
                    last = nc.tensor.transpose(bank[2 + q % 6][:, k * P:k * P + nb],
                                               rowsf[0:nb, n, :].rearrange("b (p j) -> b j p", j=TILES)[:, j0 + k, :],
                                               ident[0:nb, 0:nb])
                last.then_inc(idx_turned, 1)
            pe.wait_ge(diag_set, 4)
            pe.wait_ge(consts_set, 10)
            pe.wait_ge(idx_taken, 3)
            for t in range(2):
                nc.tensor.matmul(bank[4][:, t * P * 2:t * P * 2 + BLK_A], ones[:, :], diag[:, 2 * t, :], start=True, stop=True)
                last = nc.tensor.matmul(bank[4][:, t * P * 2 + BLK_A:t * P * 2 + BLOCKS], ones[0:BLK_B, :],
                                        diag[0:BLK_B, 2 * t + 1, 0:BLK_B], start=True, stop=True)
            last.then_inc(idx_turned, 1)
            pe.wait_ge(least_set, PASSED_SET)
            nc.tensor.matmul(bank[1][:, 0:ROUNDS], ones[0:CHUNKS, :], passed[:, :], start=True, stop=True).then_inc(idx_turned, 1)
            pe.wait_ge(weights_in, 16 * WEIGHT_DMAS)
            pe.wait_ge(be_split, 9)
            pe.wait_ge(idx_taken, 9)
            pe.wait_ge(meta_set, 3)

            rounds = Rounds(pe, "pe", META_DUE + 1)

            def turn_edges(u, s, uses, F):
                pe.wait_ge(ea_in[u], uses * 16 + 16)
                pe.wait_ge(eaT_ready, s + RING)
                rows = HALF * F
                for h in range(2):
                    last = nc.tensor.transpose(ps_eaT[0:rows, h * P:(h + 1) * P],
                                               ea[:, u, h * rows:(h + 1) * rows], ident[:, :])
                last.then_inc(eaT_made, 1)

            def features0(b, u, s):
                pe.wait_ge(eaT_ready, s + (RING + 1))
                for h in range(2):
                    pe.wait_ge(joined, s * 2 + (RING + h - 1))
                    nc.tensor.matmul(ps_feat[h][:, 0:HALF * D], pick3[:, :], be_rows[:, :], start=True, stop=False)
                    nc.tensor.matmul(ps_feat[h][:, 0:HALF * D], eaT[:, u % 2, h * P:(h + 1) * P], We_diag[:, :],
                                     start=False, stop=True).then_inc(feat_made, 1)

            def features1(b, u, s):
                pe.wait_ge(eaT_ready, s + (RING + 1))
                for h in range(2):
                    pe.wait_ge(hT_ready, b * 2 + (RING + h - 1))
                    for k in range(HALF):
                        last = nc.tensor.matmul(ps_h[h][0:D, k * P:(k + 1) * P], V1_pad[:, k, :],
                                                eaT[0:HALF * F1, u % 2, h * P:(h + 1) * P], start=True, stop=True)
                    last.then_inc(h_made, 1)
                for h in range(2):
                    pe.wait_ge(hT_ready, b * 2 + (RING + h + 1))
                    pe.wait_ge(joined, s * 2 + (RING + h - 1))
                    for k in range(HALF):
                        j = h * HALF + k
                        last = nc.tensor.matmul(ps_feat[h][:, k * D:(k + 1) * D], hT[:, j * P:(j + 1) * P], V2_s[:, :],
                                                start=True, stop=True)
                    last.then_inc(feat_made, 1)

            def aggregate(u, s, lo, hi, messages_ready):
                def window(of):
                    for j in range(TILES):
                        if j % HALF == 0:
                            messages_ready(s, j // HALF)
                        last = nc.tensor.matmul(ps_agg[0:D, 0:WINDOW], g[:, u, j * D:(j + 1) * D], of[:, j, :],
                                                start=(j == 0), stop=(j == TILES - 1))
                    return last
                with pe.If(hi >= lo + WINDOW):
                    with pe.Fori(lo + WINDOW, hi + 1, WINDOW) as w:
                        pe.wait_ge(far_onehot, rounds.next_far())
                        window(onehot_far).then_inc(far_made, 1)
                    pe.wait_ge(far_added, pe.snap(rounds.far, min_val=1))
                pe.wait_ge(onehot_ready, s + (RING + 1))
                pe.wait_ge(agg_added, s + RING)
                window(onehot).then_inc(agg_made, 1)

            def chunk_turn(layer, n):
                pe.wait_ge(ck_rows_in, n * 32 + 32)
                pe.wait_ge(ck_out_ready, n + 1)
                for k in range(KN):
                    last = nc.tensor.transpose(ps_ck[0:D, k * PN:(k + 1) * PN], ck_rows[:, k * D:(k + 1) * D],
                                               ident[0:PN, 0:PN])
                last.then_inc(ck_turned, 1)

            def chunk_first_product(layer, c, n):
                pe.wait_ge(ck_in_ready, n + 1)
                pe.wait_ge(ck_mid_ready, n + 1)
                to = ps_ck_mid[0:D, 0:CHUNK]
                if layer == 0:
                    nc.tensor.matmul(to, W1_s[:, :], ck_in[:, :], start=True, stop=True).then_inc(ck_mid_made, 1)
                else:
                    nc.tensor.matmul(to, Wn_s[:, :], aggB[:, chunk_cols(c)], start=True, stop=False)
                    nc.tensor.matmul(to, Ws_s[:, :], ck_in[:, :], start=False, stop=True).then_inc(ck_mid_made, 1)

            def chunk_last(layer, n):
                pe.wait_ge(ck_mid_ready, n + 2)
                if layer == 0:
                    nc.tensor.matmul(ps_ck[0:D, 0:CHUNK], W2_s[:, :], ck_mid[:, :], start=True, stop=True).then_inc(ck_out_made, 1)
                else:
                    for k in range(KN):
                        last = nc.tensor.transpose(ps_ck[0:PN, k * D:(k + 1) * D], ck_mid[:, k * PN:(k + 1) * PN],
                                                   ident[0:D, 0:D])
                    last.then_inc(ck_out_made, 1)

            def edges(layer, F, features, messages_ready):
                rounds.start_layer()
                turn_edges(0, layer * BLOCKS, layer * ROUNDS, F)
                features(0, 0, layer * BLOCKS)
                turn_edges(1, layer * BLOCKS + 1, layer * ROUNDS, F)

                def one_round(t):
                    rounds.load(t)
                    for u in range(RING):
                        final = isinstance(t, int)
                        s = t * RING + (u + layer * BLOCKS)
                        aggregate(u, s, *rounds.reach(u), messages_ready)
                        if not (final and u == RING - 1):
                            features(t * RING + (u + 1), (u + 1) % RING, s + 1)
                        if not (final and u >= RING - 2):
                            turn_edges((u + 2) % RING, s + 2, t + (layer * ROUNDS + (u + 2) // RING), F)
                        if u < 3:
                            with pe.If(rounds.due() >= rounds.next_chunk() + 1):
                                c = rounds.due_chunk()
                                n = c + layer * CHUNKS
                                if u == 0:
                                    chunk_turn(layer, n)
                                if u == 1:
                                    chunk_first_product(layer, c, n)
                                if u == 2:
                                    chunk_last(layer, n)
                                    rounds.chunk_done()

                with pe.Fori(0, ROUNDS - 1) as t:
                    one_round(t)
                one_round(ROUNDS - 1)
                pe.wait_ge(agg_added, RING + (layer + 1) * BLOCKS)
                with pe.If(rounds.next_chunk() < CHUNKS):
                    with pe.Fori(rounds.next_chunk(), CHUNKS) as c:
                        n = c + layer * CHUNKS
                        chunk_turn(layer, n)
                        chunk_first_product(layer, c, n)
                        chunk_last(layer, n)

            edges(0, F0, features0, lambda s, h: pe.wait_ge(msg_ready, s * 2 + (RING + h + 1)))

            def turn_back(c, u):
                v = u % 2
                pe.wait_ge(z_ready, c + 1)
                chunk_reuse(pe, y_ready, c)
                for k in range(KN):
                    last = nc.tensor.transpose(ps_row[v][0:PN, k * D:(k + 1) * D], z[:, v, k * PN:(k + 1) * PN],
                                               ident[0:D, 0:D])
                last.then_inc(row_made, 1)
            each_chunk(pe, turn_back)

            edges(1, F1, features1, lambda s, h: pe.wait_ge(joined, s * 2 + (RING + h + 1)))

        @block.scalar
        def _(act):
            def permuted(t):
                return t.rearrange("d (k p) -> d k p", k=KN)

            def by_node(t):
                return t.rearrange("d (p k) -> d k p", k=KN)

            nc.scalar.memzero(aggA[:, :]).then_inc(tables_zeroed, 1)
            nc.scalar.memzero(aggB[:, :]).then_inc(tables_zeroed, 1)
            act.wait_ge(consts_set, 10)
            act.wait_ge(weights_in, 16 * WEIGHT_DMAS)
            act.wait_ge(meta_set, 3)
            rounds = Rounds(act, "act", 1)

            def edge_features(u, s, rows, read_by, read_count):
                act.wait_ge(eaT_made, s + (RING + 1))
                act.wait_ge(read_by, read_count)
                nc.scalar.copy(eaT[0:rows, u % 2, :], ps_eaT[0:rows, 0:2 * P]).then_inc(eaT_ready, 1)

            def hidden0(n):
                act.wait_ge(ck_mid_made, n + 2)
                act.wait_ge(ck_out_made, n + 1)
                nc.scalar.activation(ck_mid[:, :], ps_ck_mid[0:D, 0:CHUNK], ACT.Relu, bias=b1_c).then_inc(ck_mid_ready, 1)

            def input1(n):
                act.wait_ge(ck_turned, n + 1)
                act.wait_ge(ck_mid_made, n + 1)
                nc.scalar.copy(by_node(ck_in[:, :]), permuted(ps_ck[0:D, 0:CHUNK])).then_inc(ck_in_ready, 1)

            def hidden1(n):
                act.wait_ge(ck_mid_made, n + 2)
                act.wait_ge(ck_out_made, n + 1)
                nc.scalar.activation(permuted(ck_mid[:, :]), by_node(ps_ck_mid[0:D, 0:CHUNK]), ACT.Relu,
                                     bias=bias_out[:, :]).then_inc(ck_mid_ready, 1)

            def deviations1(c):
                act.wait_ge(ck_lnmv_ready, c + 1)
                nc.scalar.activation(ck_lnsd[:, :], ck_lnmv[:, :, 1], ACT.Sqrt, bias=eps_c[0:PN, :]).then_inc(ck_lnsd_ready, 1)

            def edges(layer, one_block, stages):
                rounds.start_layer()
                with act.Fori(0, ROUNDS) as t:
                    rounds.load(t, META_DUE)
                    for u in range(RING):
                        one_block(t * RING + u, u, t * RING + (u + layer * BLOCKS))
                        if u in stages:
                            with act.If(rounds.due() >= rounds.next_chunk() + 1):
                                c = rounds.due_chunk()
                                stages[u](c, c + layer * CHUNKS)
                                if u == max(stages):
                                    rounds.chunk_done()
                with act.If(rounds.next_chunk() < CHUNKS):
                    with act.Fori(rounds.next_chunk(), CHUNKS) as c:
                        for u in sorted(stages):
                            stages[u](c, c + layer * CHUNKS)

            def block0(b, u, s):
                edge_features(u, s, HALF * F0, feat_made, s * 2 + (RING - 2))
                for h in range(2):
                    half = g[:, u, h * HALF * D:(h + 1) * HALF * D]
                    act.wait_ge(joined, s * 2 + (RING + h + 1))
                    nc.scalar.activation(half, half, ACT.Relu).then_inc(msg_ready, 1)

            def block1(b, u, s):
                edge_features(u, s, HALF * F1, h_made, b * 2 + (RING - 2))
                for h in range(2):
                    act.wait_ge(h_made, b * 2 + (RING + h + 1))
                    act.wait_ge(feat_made, s * 2 + (RING + h - 1))
                    nc.scalar.activation(hT[0:D, h * HALF * P:(h + 1) * HALF * P], ps_h[h][0:D, :], ACT.Relu,
                                         bias=c1_c).then_inc(hT_ready, 1)

            edges(0, block0, {2: lambda c, n: hidden0(n)})

            def normalize_roots(c, u):
                act.wait_ge(lnmv_ready, c + 1)
                nc.scalar.activation(lnsd[:, u, :], lnmv[:, u, :, 1], ACT.Sqrt, bias=eps_c[0:PN, :]).then_inc(lnsd_ready, 1)

            act.wait_ge(bn_step, 1)
            nc.scalar.activation(bn_tmp[:, 0:1], bnmv[:, 1:2], ACT.Sqrt, bias=eps_c[0:D, :]).then_inc(bn_step, 1)
            act.wait_ge(bn_step, 6)

            def batch_norm(c, u):
                v = u % 2
                chunk_reuse(act, row_made, c)
                nc.scalar.activation(permuted(z[:, v, :]), by_node(aggA[:, chunk_cols(c)]),
                                     ACT.Relu, bias=shift_bn[:, :], scale=scale_bn[:, :]).then_inc(z_ready, 1)
                if lag(c, 2):
                    normalize_roots(c - 2, (u - 2) % RING)
                if lag(c, 3):
                    normalize_rest(c - 3, (u - 3) % RING)

            def normalize_rest(c, u):
                act.wait_ge(lnnb_ready, c + 1)
                if lag(c, RING):
                    act.wait_ge(stored[u], uses_before(c, u))
                for k in range(POOL_KN, KN):
                    last = nc.scalar.activation(yn[:, u, k * D:(k + 1) * D], y[:, u, k * D:(k + 1) * D], ACT.Identity,
                                                bias=lnnb[:, u, k:k + 1], scale=lnrs[:, u, k:k + 1])
                last.then_inc(yn_ready_act, 1)
            each_chunk(act, batch_norm)
            for c in (CHUNKS - 2, CHUNKS - 1):
                normalize_roots(c, c % RING)
            for c in (CHUNKS - 3, CHUNKS - 2, CHUNKS - 1):
                normalize_rest(c, c % RING)

            edges(1, block1, {1: lambda c, n: input1(n), 2: lambda c, n: hidden1(n), 3: lambda c, n: deviations1(c)})

        @block.vector
        def _(dve):
            src_v = src_all[:, :].rearrange("p (b j) -> p b j", j=TILES)
            rel_v = rel_all[:, :].rearrange("p (b j) -> p b j", j=TILES)
            for n in range(4):
                nb = BLK_B if n % 2 else BLK_A
                dve.wait_ge(idx_rows_in[n], 48 if n % 2 else 16)
                nc.vector.tensor_copy(rowsf[0:nb, n, :], raw[n]).then_inc(rows_cast, 1)
                if n == 1:
                    for q in range(4):
                        m, j0 = IDX_GROUPS[q]
                        b0, nb = (BLK_A, BLK_B) if m % 2 else (0, BLK_A)
                        dve.wait_ge(idx_turned, q + 1)
                        nc.vector.tensor_copy(src_v[:, b0:b0 + nb, j0:j0 + HALF],
                                              bank[2 + q % 6][:, :].rearrange("p (j b) -> p b j", j=HALF)[:, 0:nb, :]
                                              ).then_inc(idx_taken, 1)
                    dve.wait_ge(idx_taken, 2)
                    nc.vector.tensor_copy(src_v[:, BLOCKS:BLOCKS + RING, :], src_v[:, 0:RING, :]).then_inc(idx_taken, 1)
            for a, nb in ((0, BLK_A), (1, BLK_B)):
                dve.wait_ge(rows_cast, 3 + a)
                for t, op in ((0, ALU.min), (1, ALU.max)):
                    nc.vector.tensor_reduce(reach[0:nb, a, t:t + 1], rowsf[0:nb, 2 + a, :], axis=AX.X, op=op).then_inc(reach_set, 1)
            dve.wait_ge(reach_set, 4)
            dve.wait_ge(consts_set, 2)
            for t in range(2):
                for a, nb in ((0, BLK_A), (1, BLK_B)):
                    nc.vector.tensor_scalar(diag[0:nb, 2 * t + a, 0:nb], ident[0:nb, 0:nb], reach[0:nb, a, t:t + 1], None,
                                            ALU.mult).then_inc(diag_set, 1)
            dve.wait_ge(idx_turned, len(IDX_GROUPS) + 1)
            nc.vector.tensor_copy(lo_all[:, :], bank[4][:, 0:BLOCKS]).then_inc(diag_set, 1)
            meta_v = meta[:, :].rearrange("o (t m) -> o t m", m=META)
            for t in range(2):
                nc.vector.tensor_copy(meta_v[:, :, t * RING:(t + 1) * RING],
                                      bank[4][0:1, t * 2 * P:t * 2 * P + BLOCKS].rearrange("o (t u) -> o t u", u=RING)
                                      ).then_inc(meta_set, 1)
            dve.wait_ge(diag_set, 5)
            nc.vector.tensor_reduce(least[:, 0, :], lo_all[0:CHUNKS, :].rearrange("p (t u) -> p t u", u=RING), axis=AX.X,
                                    op=ALU.min).then_inc(least_set, 1)
            for q in range(4, 8):
                m, j0 = IDX_GROUPS[q]
                b0, nb = (BLK_A, BLK_B) if m % 2 else (0, BLK_A)
                for k in range(HALF):
                    last = nc.vector.tensor_tensor(rel_v[:, b0:b0 + nb, j0 + k], bank[2 + q % 6][:, k * P:k * P + nb],
                                                   lo_all[:, b0:b0 + nb], ALU.subtract)
                last.then_inc(idx_taken, 1)
            for n, shift in enumerate(SHIFTS):
                a, b = least[:, n % 2, :], least[:, (n + 1) % 2, :]
                dve.wait_ge(least_set, 2 * n + 1)
                nc.vector.tensor_copy(b[:, ROUNDS - shift:], a[:, ROUNDS - shift:]).then_inc(least_set, 1)
                nc.vector.tensor_tensor(b[:, 0:ROUNDS - shift], a[:, 0:ROUNDS - shift], a[:, shift:], ALU.min).then_inc(least_set, 1)
            dve.wait_ge(least_set, 2 * len(SHIFTS) + 1)
            dve.wait_ge(consts_set, 10)
            nc.vector.tensor_scalar(passed[:, :], least[:, len(SHIFTS) % 2, :], chunk_end[:, :], None,
                                    ALU.is_ge).then_inc(least_set, 1)
            dve.wait_ge(idx_turned, len(IDX_GROUPS) + 2)
            nc.vector.tensor_copy(meta_v[:, :, META_DUE], bank[1][0:1, 0:ROUNDS]).then_inc(meta_set, 1)
            dve.wait_ge(idx_taken, 9)
            nc.vector.memset(rel_v[0:SHARED, BLOCKS - 1, :], -1.0).then_inc(tables_zeroed, 1)
            dve.wait_ge(weights_in, 16 * WEIGHT_DMAS)
            nc.vector.tensor_tensor(bias_out[:, :], bs_c, bn_c, ALU.add).then_inc(bias_set, 1)
            for k in range(3):
                nc.vector.tensor_copy(be_part[:, k, :], be_left[:, k, :]).then_inc(be_split, 1)
                dve.wait_ge(be_split, 2 * k + 1)
                if k < 2:
                    nc.vector.tensor_tensor(be_left[:, k + 1, :], be_left[:, k, :], be_part[:, k, :], ALU.subtract).then_inc(be_split, 1)
                    dve.wait_ge(be_split, 2 * k + 2)
            nc.vector.tensor_scalar(be_left[:, 0, :], be_part[:, 0, :], ident[0:3, 0:1], None, ALU.mult).then_inc(be_split, 1)
            for k in (1, 2):
                dve.wait_ge(be_split, 5 + k)
                nc.vector.scalar_tensor_tensor(out=be_left[:, k, :], in0=be_part[:, k, :], scalar=ident[0:3, k:k + 1],
                                               in1=be_left[:, k - 1, :], op0=ALU.mult, op1=ALU.add).then_inc(be_split, 1)
            dve.wait_ge(be_split, 8)
            nc.vector.tensor_copy(be_rows[0:3, :], be_left[:, 2, :]).then_inc(be_split, 1)
            dve.wait_ge(tables_zeroed, 3)
            dve.wait_ge(meta_set, 3)
            rounds = Rounds(dve, "dve", META_DUE + 1)

            def input0(c, n):
                dve.wait_ge(ck_turned, n + 1)
                dve.wait_ge(ck_mid_made, n + 1)
                nc.vector.tensor_tensor(ck_in[:, :].rearrange("d (p k) -> d k p", k=KN),
                                        ps_ck[0:D, 0:CHUNK].rearrange("d (k p) -> d k p", k=KN),
                                        aggA[:, chunk_cols(c)].rearrange("d (p k) -> d k p", k=KN),
                                        ALU.add).then_inc(ck_in_ready, 1)

            def result0(c, n):
                chunk = aggA[:, chunk_cols(c)]
                dve.wait_ge(ck_out_made, n + 2)
                nc.vector.tensor_scalar(chunk, ps_ck[0:D, 0:CHUNK], b2_c, None, ALU.add).then_inc(ck_out_ready, 1)
                dve.wait_ge(ck_out_ready, n + 2)
                nc.vector.bn_stats(bnst[:, ds(c * 6, 6)], chunk).then_inc(stats_ready, 1)

            def result1(c, n):
                dve.wait_ge(ck_out_made, n + 2)
                nc.vector.tensor_tensor(ck_y[:, :], ps_ck[0:PN, 0:KN * D], ck_rows[:, :], ALU.add).then_inc(ck_out_ready, 1)
                dve.wait_ge(ck_out_ready, n + 2)
                for k in range(KN):
                    last = nc.vector.bn_stats(ck_lnst[:, 6 * k:6 * k + 6], ck_y[:, k * D:(k + 1) * D])
                last.then_inc(ck_lnst_ready, 1)
                dve.wait_ge(ck_lnst_ready, c + 1)
                dve.sem_inc(dve_waited, 1)
                for k in range(KN):
                    last = nc.vector.bn_aggr(ck_lnmv[:, k, :], ck_lnst[:, 6 * k:6 * k + 6])
                last.then_inc(ck_lnmv_ready, 1)

            def normalized1(c, n):
                dve.wait_ge(ck_lnsd_ready, c + 1)
                nc.vector.reciprocal(ck_lnrs[:, :], ck_lnsd[:, :]).then_inc(ck_lnrs_ready, 1)
                dve.wait_ge(ck_lnrs_ready, c + 1)
                nc.vector.scalar_tensor_tensor(out=ck_lnnb[:, :], in0=ck_lnmv[:, :, 0], scalar=-1.0, in1=ck_lnrs[:, :],
                                               op0=ALU.mult, op1=ALU.mult).then_inc(ck_lnnb_ready, 1)
                dve.wait_ge(ck_lnnb_ready, c + 1)
                dve.wait_ge(ck_yn_free, c + 1)
                for k in range(KN):
                    last = nc.vector.tensor_scalar(ck_yn[:, k * D:(k + 1) * D], ck_y[:, k * D:(k + 1) * D],
                                                   ck_lnrs[:, k:k + 1], ck_lnnb[:, k:k + 1], ALU.mult, ALU.add)
                last.then_inc(ck_yn_ready, 1)

            def edges(layer, op, early, late):
                agg = (aggA, aggB)[layer]
                rounds.start_layer()

                def build_onehot(to, of):
                    for j in range(TILES):
                        last = nc.vector.tensor_scalar(to[:, j, :], iota_row[:, :], of[:, j:j + 1], None, ALU.is_equal)
                    return last

                def add_window(start):
                    return nc.vector.tensor_tensor(agg[:, ds(start, WINDOW)], ps_agg[0:D, 0:WINDOW],
                                                   agg[:, ds(start, WINDOW)], ALU.add)

                with dve.Fori(0, ROUNDS) as t:
                    rounds.load(t)
                    for u in range(RING):
                        b = t * RING + u
                        s = t * RING + (u + layer * BLOCKS)
                        lo, hi = rounds.reach(u)
                        nc.vector.tensor_copy(rel[:, :], rel_all[:, ds(b * TILES, TILES)]).then_inc(rel_set, 1)
                        nc.vector.tensor_copy(rel_far[:, :], rel_all[:, ds(b * TILES, TILES)]).then_inc(rel_set, 1)
                        dve.wait_ge(rel_set, s * 2 + (RING + 2))
                        build_onehot(onehot, rel).then_inc(onehot_ready, 1)
                        if u in early:
                            with dve.If(rounds.due() >= rounds.next_chunk() + 1):
                                c = rounds.due_chunk()
                                early[u](c, c + layer * CHUNKS)
                        for h in range(2):
                            half = g[:, u, h * HALF * D:(h + 1) * HALF * D]
                            dve.wait_ge(feat_made, s * 2 + (RING + h + 1))
                            dve.wait_ge(rows_in[u][h], t * (16 * HALF) + (layer * ROUNDS + 1) * (16 * HALF))
                            nc.vector.tensor_tensor(half, ps_feat[h][:, 0:HALF * D], half, op).then_inc(joined, 1)
                        nc.vector.tensor_copy(idx[:, u, :], src_all[:, ds((b + RING) * TILES, TILES)]).then_inc(idx_ready, 1)
                        with dve.If(hi >= lo + WINDOW):
                            with dve.Fori(lo + WINDOW, hi + 1, WINDOW) as w:
                                f = rounds.next_far()
                                nc.vector.tensor_scalar(rel_far[:, :], rel_far[:, :], -float(WINDOW), None,
                                                        ALU.add).then_inc(far_rel_set, 1)
                                dve.wait_ge(far_rel_set, f)
                                build_onehot(onehot_far, rel_far).then_inc(far_onehot, 1)
                                dve.wait_ge(far_made, f)
                                add_window(w).then_inc(far_added, 1)
                                dve.wait_ge(far_added, f)
                        dve.wait_ge(agg_made, s + (RING + 1))
                        add_window(lo).then_inc(agg_added, 1)
                        dve.wait_ge(agg_added, s + (RING + 1))
                        if u in late or u == RING - 1:
                            with dve.If(rounds.due() >= rounds.next_chunk() + 1):
                                if u in late:
                                    c = rounds.due_chunk()
                                    late[u](c, c + layer * CHUNKS)
                                if u == RING - 1:
                                    rounds.chunk_done()
                with dve.If(rounds.next_chunk() < CHUNKS):
                    with dve.Fori(rounds.next_chunk(), CHUNKS) as c:
                        for stage in (*early.values(), *late.values()):
                            stage(c, c + layer * CHUNKS)

            edges(0, ALU.add, {1: input0, 3: result0}, {})

            dve.wait_ge(stats_ready, CHUNKS)
            nc.vector.bn_aggr(bnmv[:, :], bnst[:, :]).then_inc(bn_step, 1)
            dve.wait_ge(bn_step, 2)
            nc.vector.reciprocal(bn_tmp[:, 1:2], bn_tmp[:, 0:1]).then_inc(bn_step, 1)
            dve.wait_ge(bn_step, 3)
            nc.vector.tensor_tensor(scale_bn[:, :], bn_tmp[:, 1:2], gamma_c, ALU.mult).then_inc(bn_step, 1)
            dve.wait_ge(bn_step, 4)
            nc.vector.scalar_tensor_tensor(out=shift_bn[:, :], in0=bnmv[:, 0:1], scalar=-1.0, in1=scale_bn[:, :],
                                           op0=ALU.mult, op1=ALU.mult).then_inc(bn_step, 1)
            dve.wait_ge(bn_step, 5)
            nc.vector.tensor_tensor(shift_bn[:, :], shift_bn[:, :], beta_c, ALU.add).then_inc(bn_step, 1)

            def add_input(n, c, u):
                dve.wait_ge(xr_in[u], 16 * (c // RING + 1) if isinstance(c, int) else (c - u) * (16 // RING) + 16)
                dve.wait_ge(row_made, n)
                dve.wait_ge(yn_ready, n)
                nc.vector.tensor_tensor(y[:, u, :], ps_row[u % 2][0:PN, 0:KN * D], xr[:, u, :], ALU.add).then_inc(y_ready, 1)

            def stats(n, u):
                dve.wait_ge(y_ready, n)
                for k in range(KN):
                    last = nc.vector.bn_stats(lnst[:, u, 6 * k:6 * k + 6], y[:, u, k * D:(k + 1) * D])
                last.then_inc(lnst_ready, 1)

            def mean_and_variance(n, u):
                dve.wait_ge(lnst_ready, n)
                dve.sem_inc(dve_waited, 1)
                for k in range(KN):
                    last = nc.vector.bn_aggr(lnmv[:, u, k, :], lnst[:, u, 6 * k:6 * k + 6])
                last.then_inc(lnmv_ready, 1)

            def inverse(n, u):
                dve.wait_ge(lnsd_ready, n)
                nc.vector.reciprocal(lnrs[:, u, :], lnsd[:, u, :]).then_inc(lnrs_ready, 1)

            def offset(n, u):
                dve.wait_ge(lnrs_ready, n)
                nc.vector.scalar_tensor_tensor(out=lnnb[:, u, :], in0=lnmv[:, u, :, 0], scalar=-1.0, in1=lnrs[:, u, :],
                                               op0=ALU.mult, op1=ALU.mult).then_inc(lnnb_ready, 1)

            def norm_chunk(c, u):
                n = c + 1
                if lag(c, 2):
                    inverse(n, (u - 2) % RING)
                add_input(n, c, u)
                if lag(c, 2):
                    offset(n, (u - 2) % RING)
                if lag(c, 1):
                    mean_and_variance(n, (u - 1) % RING)
                stats(n, u)
            each_chunk(dve, norm_chunk)
            mean_and_variance(CHUNKS + 1, (CHUNKS - 1) % RING)
            for c in (CHUNKS - 2, CHUNKS - 1):
                inverse(c + 3, c % RING)
                offset(c + 3, c % RING)

            edges(1, ALU.mult, {3: result1}, {3: normalized1})


_INS = ['x', 'src', 'dst', 'edge_attr_17', 'edge_attr_32', 'L0_gnn_We', 'L0_gnn_be', 'L0_gnn_W1', 'L0_gnn_b1',
        'L0_gnn_W2', 'L0_gnn_b2', 'L0_gnn_gamma', 'L0_gnn_beta', 'L1_gnn_W1', 'L1_gnn_b1', 'L1_gnn_W2', 'L1_gnn_b2',
        'L1_gnn_Ws', 'L1_gnn_bs', 'L1_gnn_Wn', 'L1_gnn_bn']
_TRANSPOSED = ('L1_gnn_W1', 'L1_gnn_W2', 'L1_gnn_Ws', 'L1_gnn_Wn')
_OUTS = [((12500, 96), 'float32')]


def kernel(**inputs):
    import numpy as _np
    import concourse.bacc as _bacc
    from concourse import mybir as _mybir
    from concourse.bass_utils import run_bass_kernel_spmd as _run

    nc = _bacc.Bacc("TRN2", target_bir_lowering=False, num_devices=1)
    arrays, args = {}, []
    for name in _INS:
        a = _np.asarray(inputs[name])
        a = _np.ascontiguousarray(a.T if name in _TRANSPOSED else a)
        arrays[f"in_{name}_dram"] = a
        args.append(nc.dram_tensor(f"in_{name}_dram", a.shape, _mybir.dt.from_np(a.dtype), kind="ExternalInput").ap())
    for i, (shape, dtype) in enumerate(_OUTS):
        dt = _mybir.dt.from_np(_np.dtype(dtype))
        args.append(nc.dram_tensor(f"out_{i}_dram", shape, dt, kind="ExternalOutput").ap())
    gnn_two_layers_kernel(nc, *args)
    r = _run(nc, [arrays], core_ids=[0])
    got = tuple(r.results[0][f"out_{i}_dram"] for i in range(len(_OUTS)))
    return got[0]
```
